# Optimizing a Trainium2 kernel written in Bass

```python
import numpy as np
import jax
import jax.numpy as jnp

def _softmax(x, axis=-1):
    return jax.nn.softmax(x, axis=axis)

def _gelu(x):
    return jax.nn.gelu(x, approximate=True)

def _silu(x):
    return jax.nn.silu(x)

def _sigmoid(x):
    return jax.nn.sigmoid(x)

def _layernorm(x, axis=-1, eps=1e-05):
    m = jnp.mean(x, axis=axis, keepdims=True)
    v = jnp.var(x, axis=axis, keepdims=True)
    return (x - m) / jnp.sqrt(v + eps)

def _scatter_add(tgt, idx, src, axis=0):
    return tgt.at[idx].add(src)

def _segment_sum(src, seg, n):
    return jax.ops.segment_sum(src, seg, n)
kernel_name = 'mk_adaln_ffn_d1_seqx_r8_42eab4'

def setup_inputs(seed: int=0):
    np.random.seed(seed)
    _w = jnp.asarray

    def _rec_inputs():
        import jax
        import jax.numpy as jnp
        _rk = jax.random.key(seed)
        x = -0.000125 + 0.9999 * jax.random.normal(jax.random.fold_in(_rk, 1), (64, 32, 512), jnp.float32)
        _lenS = 32 - jax.random.randint(jax.random.fold_in(_rk, 7), (64,), 0, max(1, 32 // 4) + 1, jnp.int32)
        _lenS2 = 32 - jax.random.randint(jax.random.fold_in(_rk, 8), (64,), 0, max(1, 32 // 4) + 1, jnp.int32)
        cond_128 = 0.0061147 + 1.02565 * jax.random.normal(jax.random.fold_in(_rk, 11), (64, 128), jnp.float32)
        return (x, cond_128)
    x, cond_128 = _rec_inputs()

    def _L0_cond_setup():
        import jax, jax.numpy as jnp
        import numpy as np
        K = 8
        T = 1.0
        D_EMBD = 128
        IN_C = 32
        OUT_C = 32
        BS = 32
        H = 512
        HID = 128
        key = jax.random.key(seed)
        ks = jax.random.split(key, 10)
        s = lambda fan_in: 1.0 / np.sqrt(fan_in)
        return {'x': jax.random.normal(ks[0], (BS, IN_C, H), dtype=jnp.float32), 'embedding': jax.random.normal(ks[1], (BS, D_EMBD), dtype=jnp.float32), 'W0': jax.random.normal(ks[2], (D_EMBD, HID), dtype=jnp.float32) * s(D_EMBD), 'b0': jnp.zeros((HID,), dtype=jnp.float32), 'W1': jax.random.normal(ks[3], (HID, HID), dtype=jnp.float32) * s(HID), 'b1': jnp.zeros((HID,), dtype=jnp.float32), 'W2': jax.random.normal(ks[4], (HID, K), dtype=jnp.float32) * s(HID), 'b2': jnp.zeros((K,), dtype=jnp.float32), 'weight': jax.random.normal(ks[5], (K, OUT_C, IN_C, 1), dtype=jnp.float32) * s(IN_C), 'bias_k': jax.random.normal(ks[6], (K, OUT_C), dtype=jnp.float32) * 0.1}
    _L0_cond_all = _L0_cond_setup()
    _L0_cond_in = {k: v for k, v in _L0_cond_all.items() if k in ('W0', 'b0', 'W1', 'b1', 'W2', 'b2', 'weight', 'bias_k')}
    del _L0_cond_all

    def _L0_ffn_setup():
        import jax, jax.numpy as jnp
        import numpy as np
        HID, INT, LAT, NE, K = (512, 1024, 256, 8, 2)
        LN_EPS = 1e-05

        def _layernorm(x, gamma, beta):
            mu = jnp.mean(x, axis=-1, keepdims=True)
            var = jnp.var(x, axis=-1, keepdims=True)
            return (x - mu) * jax.lax.rsqrt(var + LN_EPS) * gamma + beta
        key = jax.random.key(seed)
        ks = jax.random.split(key, 8)
        s = lambda d: 1.0 / np.sqrt(d)
        return {'hidden_states': jax.random.normal(ks[0], (4, 256, HID), jnp.float32), 'gate_w': jax.random.normal(ks[1], (HID, NE), jnp.float32) * s(HID), 'up_w': jax.random.normal(ks[2], (HID, INT), jnp.float32) * s(HID), 'down_w': jax.random.normal(ks[3], (INT, HID), jnp.float32) * s(INT), 'fc1_w': jax.random.normal(ks[4], (HID, LAT), jnp.float32) * s(HID), 'fc2_w': jax.random.normal(ks[5], (LAT, HID), jnp.float32) * s(LAT), 'expert_w': jax.random.normal(ks[6], (LAT, LAT), jnp.float32), 'ln_gamma': jnp.ones((HID,), jnp.float32), 'ln_beta': jnp.zeros((HID,), jnp.float32)}
    _L0_ffn_all = _L0_ffn_setup()
    _L0_ffn_in = {k: v for k, v in _L0_ffn_all.items() if k in ('gate_w', 'up_w', 'down_w', 'fc1_w', 'fc2_w', 'expert_w', 'ln_gamma', 'ln_beta')}
    del _L0_ffn_all
    return {'x': x, 'cond_128': cond_128, 'L0_cond_W0': _L0_cond_in['W0'], 'L0_cond_b0': _L0_cond_in['b0'], 'L0_cond_W1': _L0_cond_in['W1'], 'L0_cond_b1': _L0_cond_in['b1'], 'L0_cond_W2': _L0_cond_in['W2'], 'L0_cond_b2': _L0_cond_in['b2'], 'L0_cond_weight': _L0_cond_in['weight'], 'L0_cond_bias_k': _L0_cond_in['bias_k'], 'L0_ffn_gate_w': _L0_ffn_in['gate_w'], 'L0_ffn_up_w': _L0_ffn_in['up_w'], 'L0_ffn_down_w': _L0_ffn_in['down_w'], 'L0_ffn_fc1_w': _L0_ffn_in['fc1_w'], 'L0_ffn_fc2_w': _L0_ffn_in['fc2_w'], 'L0_ffn_expert_w': _L0_ffn_in['expert_w'], 'L0_ffn_ln_gamma': _L0_ffn_in['ln_gamma'], 'L0_ffn_ln_beta': _L0_ffn_in['ln_beta']}

def reference(x, cond_128, L0_cond_W0, L0_cond_b0, L0_cond_W1, L0_cond_b1, L0_cond_W2, L0_cond_b2, L0_cond_weight, L0_cond_bias_k, L0_ffn_gate_w, L0_ffn_up_w, L0_ffn_down_w, L0_ffn_fc1_w, L0_ffn_fc2_w, L0_ffn_expert_w, L0_ffn_ln_gamma, L0_ffn_ln_beta):
    import jax
    import jax.numpy as jnp

    def _L0_cond_ref(x, embedding, W0, b0, W1, b1, W2, b2, weight, bias_k):
        import jax, jax.numpy as jnp
        import numpy as np
        K = 8
        T = 1.0
        D_EMBD = 128
        IN_C = 32
        OUT_C = 32
        BS = 32
        H = 512
        HID = 128
        h = jax.nn.gelu(embedding @ W0 + b0, approximate=False)
        h = jax.nn.gelu(h @ W1 + b1, approximate=False)
        att = jax.nn.softmax((h @ W2 + b2) / T, axis=-1)
        agg_w = jnp.einsum('bk,koi->boi', att, weight[..., 0])
        agg_b = att @ bias_k
        out = jnp.einsum('boi,bih->boh', agg_w, x) + agg_b[:, :, None]
        return out

    def _L0_ffn_ref(hidden_states, gate_w, up_w, down_w, fc1_w, fc2_w, expert_w, ln_gamma, ln_beta):
        import jax, jax.numpy as jnp
        import numpy as np
        HID, INT, LAT, NE, K = (512, 1024, 256, 8, 2)
        LN_EPS = 1e-05

        def _layernorm(x, gamma, beta):
            mu = jnp.mean(x, axis=-1, keepdims=True)
            var = jnp.var(x, axis=-1, keepdims=True)
            return (x - mu) * jax.lax.rsqrt(var + LN_EPS) * gamma + beta
        logits = jnp.einsum('bsh,he->bse', hidden_states, gate_w)
        routing_weights, selected_experts = jax.lax.top_k(logits, K)
        h = jax.nn.relu(jnp.einsum('bsh,hi->bsi', hidden_states, up_w)) ** 2
        shared_out = jnp.einsum('bsi,ih->bsh', h, down_w)
        x_latent = jnp.einsum('bsh,hl->bsl', hidden_states, fc1_w)
        expert_out = jnp.einsum('bsl,lm->bsm', x_latent, expert_w)
        moe_out = expert_out * jnp.sum(routing_weights, axis=-1, keepdims=True)
        routed_out = jnp.einsum('bsl,lh->bsh', moe_out, fc2_w)
        return _layernorm(shared_out + routed_out, ln_gamma, ln_beta)
    x = x + _L0_ffn_ref(_L0_cond_ref(x, cond_128, L0_cond_W0, L0_cond_b0, L0_cond_W1, L0_cond_b1, L0_cond_W2, L0_cond_b2, L0_cond_weight, L0_cond_bias_k), L0_ffn_gate_w, L0_ffn_up_w, L0_ffn_down_w, L0_ffn_fc1_w, L0_ffn_fc2_w, L0_ffn_expert_w, L0_ffn_ln_gamma, L0_ffn_ln_beta)
    return x

_drawn_inputs = setup_inputs


def setup_inputs(seed=0):
    import zlib

    import numpy as np

    out = dict(_drawn_inputs(seed))
    spreads = {'L0_cond_b0': (0.0, 0.1),
     'L0_cond_b1': (0.0, 0.1),
     'L0_cond_b2': (0.0, 0.1),
     'L0_ffn_ln_gamma': (1.0, 0.2),
     'L0_ffn_ln_beta': (0.0, 0.1)}
    factors = {}
    for name, (base, spread) in spreads.items():
        noise = np.random.default_rng([zlib.crc32(name.encode()), seed]).standard_normal(out[name].shape)
        drawn = base * np.exp(spread * noise) if base else spread * noise
        out[name] = jnp.asarray(drawn.astype(out[name].dtype))
    for name, factor in factors.items():
        out[name] = (out[name] * factor).astype(out[name].dtype)
    return out
```

```python
import concourse.bass as bass
from concourse import mybir
from contextlib import ExitStack


def adaln_ffn_kernel(
    nc: bass.Bass,
    x: bass.AP,
    cond: bass.AP,
    W0: bass.AP,
    b0: bass.AP,
    W1: bass.AP,
    b1: bass.AP,
    W2: bass.AP,
    b2: bass.AP,
    weight: bass.AP,
    bias_k: bass.AP,
    gate_w: bass.AP,
    up_w: bass.AP,
    down_w: bass.AP,
    fc1_w: bass.AP,
    fc2_w: bass.AP,
    expert_w: bass.AP,
    gamma: bass.AP,
    beta: bass.AP,
    out: bass.AP,
):
    fp32 = mybir.dt.float32
    f32r = mybir.dt.float32r
    ALU = mybir.AluOpType
    ACT = mybir.ActivationFunctionType
    AX = mybir.AxisListType

    NB, C, HID = x.shape
    D = cond.shape[1]
    K = W2.shape[1]
    NE = gate_w.shape[1]
    INT = up_w.shape[1]
    LAT = fc1_w.shape[1]
    P = 128
    G = P // C
    NT = NB // G
    TB = 4
    TOK = TB * P
    NBLK = NT // TB
    HC, IC, LC = HID // P, INT // P, LAT // P
    EPS = 1e-5
    WB = 4
    UPC = INT // 4
    DNC = IC // 4
    SC = 512

    UP_BANK = [m % WB for m in range(IC)]
    LAT_BANK = [0, 1]
    GATE_BANK = 2
    MIX_BANK = [3, 0, 2, 3]
    TOP_BANK = 1

    x_v = x.rearrange("(n g) c h -> (g c) n h", g=G)
    out_v = out.rearrange("(n g) c h -> (g c) n h", g=G)
    up_v = up_w.rearrange("(k p) n -> p k n", p=P)
    down_v = down_w.rearrange("(k p) n -> p k n", p=P)
    fc1_v = fc1_w.rearrange("(k p) n -> p k n", p=P)
    fc2_v = fc2_w.rearrange("(k p) n -> p k n", p=P)
    expert_v = expert_w.rearrange("(k p) n -> p k n", p=P)
    gate_v = gate_w.rearrange("(k p) n -> p k n", p=P)

    ctx = ExitStack()
    with ctx:
        def sb(name, shape, dt=fp32):
            return ctx.enter_context(nc.sbuf_tensor(name, shape, dt))

        def sem(name):
            return ctx.enter_context(nc.semaphore(name))

        up_hi = sb("up_hi", [P, HC, INT], f32r)
        up_lo = sb("up_lo", [P, HC, INT], f32r)
        down_hi = sb("down_hi", [P, IC, HID], f32r)
        down_lo = sb("down_lo", [P, IC, HID], f32r)
        fc1_hi = sb("fc1_hi", [P, HC, LAT], f32r)
        fc1_lo = sb("fc1_lo", [P, HC, LAT], f32r)
        q_hi = sb("q_hi", [P, LC, HID], f32r)
        q_lo = sb("q_lo", [P, LC, HID], f32r)
        gate_hl = sb("gate_hl", [P, HC, P], f32r)

        h_hi = sb("h_hi", [P, HC, TOK], f32r)
        h_lo = sb("h_lo", [P, HC, TOK], f32r)
        sq_hi = sb("sq_hi", [P, IC, TOK], f32r)
        sq_lo = sb("sq_lo", [P, IC, TOK], f32r)
        lat_hi = sb("lat_hi", [P, LC, TOK], f32r)
        lat_lo = sb("lat_lo", [P, LC, TOK], f32r)
        x_cur = sb("x_cur", [P, TB, HID])
        h_full = sb("h_full", [P, 2, TOK])
        relu_sq = sb("relu_sq", [P, 2, TOK])
        y_buf = sb("y_buf", [P, 2, HID])
        late = sb("late", [P, IC * HID])
        up_raw = late[:, :].rearrange("p (k n) -> p k n", k=HC)
        down_raw = late[:, :].rearrange("p (k n) -> p k n", k=IC)
        x_beta = late[:, 0:TB * HID].rearrange("p (t n) -> p t n", t=TB)
        out_buf = late[:, TB * HID:2 * TB * HID].rearrange("p (t n) -> p t n", t=TB)
        top8 = sb("top8", [P, TB, NE])
        top2 = sb("top2", [P, TB])
        stats = sb("stats", [P, 6])
        mv = sb("mv", [P, 2])
        rstd = sb("rstd", [P, 1])

        agg = sb("agg", [P, NT, C])
        mix = sb("mix", [P, TB, P])
        agg_b = sb("agg_b", [P, NB * C])
        gamma_b = sb("gamma_b", [P, HID])
        beta_b = sb("beta_b", [P, HID])

        fc1_raw = sb("fc1_raw", [P, HC, LAT])
        fc2_raw = sb("fc2_raw", [P, LC, HID])
        expert_raw = sb("expert_raw", [P, LC, LAT])
        gate_sb = expert_raw[0:2 * NE, :, :].rearrange("p k n -> p (k n)")
        expert_T = sb("expert_T", [P, LC, LAT])
        gate_raw = sb("gate_raw", [P, HC, NE])
        cond_in = sb("cond_in", [NB, D])
        cond_T = sb("cond_T", [D, NB])
        w0_sb = sb("w0_sb", [D, D])
        w1_sb = sb("w1_sb", [D, D])
        w2_sb = sb("w2_sb", [D, K])
        b0_sb = sb("b0_sb", [D, 1])
        b1_sb = sb("b1_sb", [D, 1])
        b2_sb = sb("b2_sb", [1, K])
        weight_sb = relu_sq[0:K, :, :].rearrange("k a n -> k (a n)")
        bias_sb = sb("bias_sb", [K, C])
        hid1 = sb("hid1", [D, NB])
        hid2 = sb("hid2", [D, NB])
        att = sb("att", [NB, K])
        att_T = sb("att_T", [K, NB])
        neg_max = sb("neg_max", [NB, 1])
        exp_sum = sb("exp_sum", [NB, 1])
        exp_inv = sb("exp_inv", [NB, 1])
        att_bias = y_buf[0:K, :, :]
        ident = sb("ident", [P, P])
        pick = sb("pick", [2 * NE, NE])
        ones = sb("ones", [K, P])
        half = sb("half", [P, 1])
        warm = sb("warm", [P, 1])

        ps = ctx.enter_context(nc.psum_tensor("ps", [P, 8, TOK], fp32))
        EMB = ps[:, 4, 0:NB]
        H1 = ps[:, 4, 64:64 + NB]
        H2 = ps[:, 4, 128:128 + NB]
        LOGIT = ps[0:NB, 4, 192:192 + K]
        ATT_T = ps[0:K, 4, 256:256 + NB]
        EXP_T = ps[:, 5, :].rearrange("p (c n) -> p c n", c=LC)
        Q = [ps[:, 6, :], ps[:, 7, :]]
        AGG = ps[:, 1, :].rearrange("p (c b) -> p c b", b=NB)
        AGG_B_BANK = [5, 4, 6, 7]

        def agg_src(q, g, tiles):
            return AGG[q * C:(q + 1) * C, :, g:tiles * G:G]

        def agg_part(g, q):
            return agg[g * C:(g + 1) * C, :, q:C:G].rearrange("i n c -> i c n")

        def mix_part(g, q):
            return mix[g * C:(g + 1) * C, :, g * C + q:(g + 1) * C:G].rearrange("i t c -> i c t")

        def shared(t):
            return ps[:, 4 + t % 2, :]

        def routed(t):
            return ps[:, 6 + t % 2, :]

        cond_loaded = sem("cond_loaded")
        w0_loaded = sem("w0_loaded")
        w1_loaded = sem("w1_loaded")
        mix_loaded = sem("mix_loaded")
        expert_loaded = sem("expert_loaded")
        fc2_loaded = sem("fc2_loaded")
        x_loaded = sem("x_loaded")
        up_loaded = [sem(f"up_loaded{i}") for i in range(4)]
        fc1_loaded = sem("fc1_loaded")
        gate_loaded = sem("gate_loaded")
        down_loaded = [sem(f"down_loaded{i}") for i in range(4)]
        affine_loaded = sem("affine_loaded")
        stored = [sem(f"stored{t}") for t in range(TB)]
        zeroed = sem("zeroed")
        const_ready = sem("const_ready")
        dve_const = sem("dve_const")
        emb_done = sem("emb_done")
        emb_copied = sem("emb_copied")
        expT_done = sem("expT_done")
        expT_copied = sem("expT_copied")
        h1_done = sem("h1_done")
        gelu_done = sem("gelu_done")
        h2_done = sem("h2_done")
        logit_done = sem("logit_done")
        max_done = sem("max_done")
        exp_done = sem("exp_done")
        inv_done = sem("inv_done")
        att_done = sem("att_done")
        attT_done = sem("attT_done")
        attT_copied = sem("attT_copied")
        agg_done = sem("agg_done")
        q_done = sem("q_done")
        q_hi_ready = sem("q_hi_ready")
        q_lo_ready = sem("q_lo_ready")
        attb_ready = sem("attb_ready")
        aggb_done = sem("aggb_done")
        aggb_copied = sem("aggb_copied")
        mix0_act = sem("mix0_act")
        mix0_dve = sem("mix0_dve")
        agg_act = sem("agg_act")
        agg_dve = sem("agg_dve")
        up_hi_ready = sem("up_hi_ready")
        up_lo_ready = sem("up_lo_ready")
        fc1_hi_ready = sem("fc1_hi_ready")
        fc1_lo_ready = sem("fc1_lo_ready")
        gate_hi_ready = sem("gate_hi_ready")
        gate_lo_ready = sem("gate_lo_ready")
        down_hi_ready = sem("down_hi_ready")
        down_lo_ready = sem("down_lo_ready")
        mix_ready = sem("mix_ready")
        mix_done = sem("mix_done")
        h_ready = sem("h_ready")
        h_hi_ready = sem("h_hi_ready")
        h_lo_ready = sem("h_lo_ready")
        up_done = sem("up_done")
        relu_done = sem("relu_done")
        square_done = sem("square_done")
        sq_hi_ready = sem("sq_hi_ready")
        sq_lo_ready = sem("sq_lo_ready")
        lat_done = sem("lat_done")
        lat_hi_ready = sem("lat_hi_ready")
        lat_lo_ready = sem("lat_lo_ready")
        gate_done = sem("gate_done")
        gate_copied = sem("gate_copied")
        logits_done = sem("logits_done")
        top8_done = sem("top8_done")
        top2_done = sem("top2_done")
        routed_done = sem("routed_done")
        scaled_done = sem("scaled_done")
        shared_done = sem("shared_done")
        y_done = sem("y_done")
        stats_done = sem("stats_done")
        mv_done = sem("mv_done")
        rstd_done = sem("rstd_done")
        gamma_done = sem("gamma_done")
        final_done = sem("final_done")
        xbeta_ready = sem("xbeta_ready")

        def wait_past(eng, semaphore, value):
            if not (isinstance(value, int) and value == 0):
                eng.wait_ge(semaphore, value)

        block = ctx.enter_context(nc.Block())

        @block.sync
        def _(sp):
            sp.dma_start(cond_in[:, :], cond).then_inc(cond_loaded, 16)
            sp.dma_start(w0_sb[:, :], W0).then_inc(w0_loaded, 16)
            sp.dma_start(w1_sb[:, :], W1).then_inc(w1_loaded, 16)
            sp.dma_start(expert_raw[:, :, :], expert_v).then_inc(expert_loaded, 16)
            sp.dma_start(fc2_raw[:, :, :], fc2_v).then_inc(fc2_loaded, 16)
            sp.dma_start(x_cur[:, :, :], x_v[:, 0:TB, :]).then_inc(x_loaded, 16)
            for i in range(4):
                sp.dma_start(up_raw[:, :, i * UPC:(i + 1) * UPC],
                             up_v[:, :, i * UPC:(i + 1) * UPC]).then_inc(up_loaded[i], 16)
            sp.dma_start(fc1_raw[:, :, :], fc1_v).then_inc(fc1_loaded, 16)
            sp.dma_start(gate_raw[:, :, :], gate_v).then_inc(gate_loaded, 16)
            sp.dma_start(gamma_b[:, :], gamma.partition_broadcast(P)).then_inc(affine_loaded, 16)
            sp.dma_start(beta_b[:, :], beta.partition_broadcast(P)).then_inc(affine_loaded, 16)
            sp.wait_ge(up_hi_ready, 4)
            sp.wait_ge(up_lo_ready, 4)
            for i in range(4):
                sp.dma_start(down_raw[:, i * DNC:(i + 1) * DNC, :],
                             down_v[:, i * DNC:(i + 1) * DNC, :]).then_inc(down_loaded[i], 16)

            def load_next_x(b):
                sp.wait_ge(mix_done, HC * (b + 1))
                sp.wait_ge(xbeta_ready, b + 1)
                sp.dma_start(x_cur[:, :, :], x_v[:, bass.ds((b + 1) * TB, TB), :]).then_inc(x_loaded, 16)

            def store_block(b):
                for t in range(TB):
                    sp.wait_ge(final_done, TB * b + t + 1)
                    sp.dma_start(out_v[:, bass.ds(b * TB + t, 1), :],
                                 out_buf[:, t:t + 1, :]).then_inc(stored[t], 16)

            with sp.Fori(0, NBLK - 1) as b:
                load_next_x(b)
                store_block(b)
            store_block(NBLK - 1)
            for t in range(TB):
                sp.wait_ge(stored[t], 16 * NBLK)

        @block.gpsimd
        def _(pool):
            nc.gpsimd.memset(ident[:, :], 0.0).then_inc(zeroed, 1)
            nc.gpsimd.memset(pick[:, :], 0.0).then_inc(zeroed, 1)
            pool.wait_ge(zeroed, 2)
            nc.gpsimd.affine_select(out=ident[:, :], in_=ident[:, :], compare_op=ALU.not_equal, fill=1.0,
                                    base=0, pattern=[[-1, P]], channel_multiplier=1).then_inc(const_ready, 1)
            nc.gpsimd.affine_select(out=pick[:, :], in_=pick[:, :], compare_op=ALU.not_equal, fill=1.0,
                                    base=0, pattern=[[-1, NE]], channel_multiplier=1).then_inc(zeroed, 1)
            pool.wait_ge(zeroed, 3)
            nc.gpsimd.affine_select(out=pick[:, :], in_=pick[:, :], compare_op=ALU.not_equal, fill=1.0,
                                    base=-NE, pattern=[[-1, NE]], channel_multiplier=1).then_inc(const_ready, 1)
            nc.gpsimd.memset(mix[:, :, :], 0.0).then_inc(const_ready, 1)
            nc.gpsimd.memset(half[:, :], -0.5).then_inc(const_ready, 1)
            pool.wait_ge(attT_copied, 1)
            pool.wait_ge(mix_loaded, 64)
            for i in range(NBLK):
                nb = SC // C
                if i >= 2:
                    pool.wait_ge(aggb_done, i - 1)
                nc.gpsimd.tensor_tensor(
                    att_bias[:, i % 2, :].rearrange("k (b o) -> k b o", o=C),
                    att_T[:, i * nb:(i + 1) * nb].unsqueeze(2).to_broadcast([K, nb, C]),
                    bias_sb[:, :].unsqueeze(1).to_broadcast([K, nb, C]), ALU.mult).then_inc(attb_ready, 1)
            pool.wait_ge(agg_act, 2 * G)
            pool.wait_ge(agg_dve, 2 * G)

            def next_mix(b):
                pool.wait_ge(mix_done, HC * (b + 1))
                pool.wait_ge(xbeta_ready, b + 1)
                for g in range(G):
                    if g > 0:
                        pool.wait_ge(mix_ready, G * b + g)
                    r = slice(g * C, (g + 1) * C)
                    nc.gpsimd.tensor_copy(mix[r, :, r], agg[r, bass.ds((b + 1) * TB, TB), :]).then_inc(mix_ready, 1)

            def x_plus_beta(b):
                pool.wait_ge(x_loaded, 16 * (b + 1))
                wait_past(pool, final_done, TB * b)
                nc.gpsimd.tensor_tensor(x_beta, x_cur[:, :, :],
                                        beta_b[:, :].unsqueeze(1).to_broadcast([P, TB, HID]),
                                        ALU.add).then_inc(xbeta_ready, 1)

            def inverse_deviations(b):
                for t in range(TB):
                    pool.wait_ge(mv_done, 2 * (TB * b + t + 1))
                    nc.gpsimd.tensor_tensor(rstd[:, :], mv[:, 1:2], half[:, :], ALU.pow).then_inc(rstd_done, 1)

            pool.wait_ge(affine_loaded, 32)
            pool.wait_ge(down_hi_ready, 4)
            pool.wait_ge(down_lo_ready, 4)
            def pool_block(b):
                x_plus_beta(b)
                next_mix(b)
                pool.wait_ge(mix_ready, G * (b + 1))
                inverse_deviations(b)

            pool_block(0)
            with pool.Fori(1, NBLK - 1) as b:
                pool_block(b)
            x_plus_beta(NBLK - 1)
            inverse_deviations(NBLK - 1)

        @block.scalar
        def _(act):
            act.dma_start(b0_sb[:, :], b0.unsqueeze(1)).then_inc(w0_loaded, 16)
            act.dma_start(b1_sb[:, :], b1.unsqueeze(1)).then_inc(w1_loaded, 16)
            act.dma_start(w2_sb[:, :], W2).then_inc(mix_loaded, 16)
            act.dma_start(b2_sb[:, :], b2.unsqueeze(0)).then_inc(mix_loaded, 16)
            act.dma_start(weight_sb, weight.rearrange("k o i u -> k (o i u)")).then_inc(mix_loaded, 16)
            act.dma_start(bias_sb[:, :], bias_k).then_inc(mix_loaded, 16)
            act.wait_ge(dve_const, 1)
            nc.scalar.activation(warm[:, :], warm[:, :], ACT.Gelu)
            act.wait_ge(w0_loaded, 32)
            act.wait_ge(h1_done, 1)
            nc.scalar.activation(hid1[:, :], H1, ACT.Gelu, bias=b0_sb[:, :]).then_inc(gelu_done, 1)
            act.wait_ge(w1_loaded, 32)
            act.wait_ge(h2_done, 1)
            nc.scalar.activation(hid2[:, :], H2, ACT.Gelu, bias=b1_sb[:, :]).then_inc(gelu_done, 1)
            act.wait_ge(logit_done, 1)
            act.wait_ge(max_done, 1)
            nc.scalar.activation(att[:, :], LOGIT, ACT.Exp, bias=neg_max[:, :],
                                 accum_out=exp_sum[:, :]).then_inc(exp_done, 1)

            def split_up(i):
                cols = slice(i * UPC, (i + 1) * UPC)
                act.wait_ge(up_loaded[i], 16)
                nc.scalar.copy(up_hi[:, :, cols], up_raw[:, :, cols]).then_inc(up_hi_ready, 1)

            def q_high(lc):
                act.wait_ge(q_done, lc + 1)
                nc.scalar.copy(q_hi[:, lc, :], Q[lc]).then_inc(q_hi_ready, 1)

            def agg_bias(i):
                act.wait_ge(aggb_done, i + 1)
                nc.scalar.copy(agg_b[:, i * SC:(i + 1) * SC], ps[:, AGG_B_BANK[i], :]).then_inc(aggb_copied, 1)

            def mix_high(b):
                for c in range(HC):
                    act.wait_ge(h_ready, HC * b + c + 1)
                    nc.scalar.copy(h_hi[:, c, :], h_full[:, c % 2, :]).then_inc(h_hi_ready, 1)

            q_high(0)
            split_up(0)
            act.wait_ge(const_ready, 3)
            act.wait_ge(agg_done, 1)
            for q in (0, 1):
                for g in range(G):
                    nc.scalar.copy(mix_part(g, q), agg_src(q, g, TB)).then_inc(mix0_act, 1)
            agg_bias(0)
            for q in (0, 1):
                for g in range(G):
                    nc.scalar.copy(agg_part(g, q), agg_src(q, g, NT)).then_inc(agg_act, 1)
            mix_high(0)
            split_up(1)
            q_high(1)
            split_up(2)
            split_up(3)
            for i in range(1, NBLK):
                agg_bias(i)
            act.wait_ge(fc1_loaded, 16)
            nc.scalar.copy(fc1_hi[:, :, :], fc1_raw[:, :, :]).then_inc(fc1_hi_ready, 1)
            act.wait_ge(gate_loaded, 16)
            act.wait_ge(dve_const, 2)
            nc.scalar.copy(gate_hl[:, :, 0:NE], gate_raw[:, :, :]).then_inc(gate_hi_ready, 1)

            def relu_square(b, m):
                act.wait_ge(up_done, IC * b + m + 1)
                wait_past(act, sq_lo_ready, IC * b + max(m - 1, 0))
                nc.scalar.activation(relu_sq[:, m % 2, :], ps[:, UP_BANK[m], :], ACT.Relu).then_inc(relu_done, 1)
                act.wait_ge(relu_done, IC * b + m + 1)
                nc.scalar.activation(relu_sq[:, m % 2, :], relu_sq[:, m % 2, :], ACT.Square).then_inc(square_done, 1)

            def latent_gate(b):
                for lc in range(LC):
                    act.wait_ge(lat_done, LC * b + lc + 1)
                    nc.scalar.copy(lat_hi[:, lc, :], ps[:, LAT_BANK[lc], :]).then_inc(lat_hi_ready, 1)
                act.wait_ge(gate_done, b + 1)
                nc.scalar.copy(gate_sb, ps[0:2 * NE, GATE_BANK, :]).then_inc(gate_copied, 1)

            def scale_routed(b):
                act.wait_ge(top2_done, b + 1)
                for t in range(TB):
                    act.wait_ge(routed_done, TB * b + t + 1)
                    wait_past(act, final_done, TB * b + max(t - 1, 0))
                    nc.scalar.mul(y_buf[:, t % 2, :], routed(t), top2[:, t:t + 1]).then_inc(scaled_done, 1)

            def down_high(i):
                ks = slice(i * DNC, (i + 1) * DNC)
                act.wait_ge(down_loaded[i], 16)
                nc.scalar.copy(down_hi[:, ks, :], down_raw[:, ks, :]).then_inc(down_hi_ready, 1)

            for m in range(IC):
                relu_square(0, m)
                if m % 2 == 1:
                    down_high(m // 2)
            latent_gate(0)
            mix_high(1)
            scale_routed(0)
            with act.Fori(1, NBLK - 1) as b:
                for m in range(IC):
                    relu_square(b, m)
                latent_gate(b)
                mix_high(b + 1)
                scale_routed(b)
            for m in range(IC):
                relu_square(NBLK - 1, m)
            latent_gate(NBLK - 1)
            scale_routed(NBLK - 1)

        @block.vector
        def _(dve):
            nc.vector.memset(warm[:, :], 0.0).then_inc(dve_const, 1)
            nc.vector.memset(gate_hl[:, :, :].bitcast(mybir.dt.uint32), 0).then_inc(dve_const, 1)
            nc.vector.memset(ones[:, :], 1.0).then_inc(dve_const, 1)
            dve.wait_ge(emb_done, 1)
            nc.vector.tensor_copy(cond_T[:, :], EMB).then_inc(emb_copied, 1)
            dve.wait_ge(expT_done, 1)
            nc.vector.tensor_copy(expert_T[:, :, :], EXP_T).then_inc(expT_copied, 1)
            dve.wait_ge(logit_done, 1)
            nc.vector.tensor_reduce(neg_max[:, :], LOGIT, AX.X, ALU.max, negate=True).then_inc(max_done, 1)
            dve.wait_ge(exp_done, 1)
            nc.vector.reciprocal(exp_inv[:, :], exp_sum[:, :]).then_inc(inv_done, 1)
            dve.wait_ge(inv_done, 1)
            nc.vector.tensor_scalar(att[:, :], att[:, :], exp_inv[:, :], None, ALU.mult).then_inc(att_done, 1)
            dve.wait_ge(attT_done, 1)
            nc.vector.tensor_copy(att_T[:, :], ATT_T).then_inc(attT_copied, 1)

            def split_up(i):
                cols = slice(i * UPC, (i + 1) * UPC)
                dve.wait_ge(up_hi_ready, i + 1)
                nc.vector.tensor_tensor(up_lo[:, :, cols], up_raw[:, :, cols],
                                        up_hi[:, :, cols].bitcast(fp32), ALU.subtract).then_inc(up_lo_ready, 1)

            def q_low(lc):
                dve.wait_ge(q_hi_ready, lc + 1)
                nc.vector.tensor_tensor(q_lo[:, lc, :], Q[lc], q_hi[:, lc, :].bitcast(fp32),
                                        ALU.subtract).then_inc(q_lo_ready, 1)

            def mix_bias(b, c):
                dve.wait_ge(mix_done, HC * b + c + 1)
                wait_past(dve, h_hi_ready, HC * b + max(c - 1, 0))
                wait_past(dve, h_lo_ready, HC * b + max(c - 1, 0))
                nc.vector.tensor_tensor(h_full[:, c % 2, :], ps[:, MIX_BANK[c], :],
                                        agg_b[:, bass.ds(b * TOK, TOK)], ALU.add).then_inc(h_ready, 1)

            def mix_low(b, c):
                dve.wait_ge(h_hi_ready, HC * b + c + 1)
                nc.vector.tensor_tensor(h_lo[:, c, :], h_full[:, c % 2, :], h_hi[:, c, :].bitcast(fp32),
                                        ALU.subtract).then_inc(h_lo_ready, 1)

            def mix_block(b):
                mix_bias(b, 0)
                for c in range(HC):
                    if c + 1 < HC:
                        mix_bias(b, c + 1)
                    mix_low(b, c)

            dve.wait_ge(const_ready, 3)
            dve.wait_ge(agg_done, 1)
            for q in (2, 3):
                for g in range(G):
                    nc.vector.tensor_copy(mix_part(g, q), agg_src(q, g, TB)).then_inc(mix0_dve, 1)
            for q in (2, 3):
                for g in range(G):
                    nc.vector.tensor_copy(agg_part(g, q), agg_src(q, g, NT)).then_inc(agg_dve, 1)
            q_low(0)
            split_up(0)
            dve.wait_ge(aggb_copied, 1)
            mix_block(0)
            split_up(1)
            q_low(1)
            split_up(2)
            split_up(3)
            dve.wait_ge(fc1_hi_ready, 1)
            nc.vector.tensor_tensor(fc1_lo[:, :, :], fc1_raw[:, :, :], fc1_hi[:, :, :].bitcast(fp32),
                                    ALU.subtract).then_inc(fc1_lo_ready, 1)
            dve.wait_ge(gate_hi_ready, 1)
            nc.vector.tensor_tensor(gate_hl[:, :, NE:2 * NE], gate_raw[:, :, :],
                                    gate_hl[:, :, 0:NE].bitcast(fp32), ALU.subtract).then_inc(gate_lo_ready, 1)
            dve.wait_ge(aggb_copied, NBLK)

            def split_square(b, m):
                dve.wait_ge(square_done, IC * b + m + 1)
                nc.vector.tensor_copy(sq_hi[:, m, :], relu_sq[:, m % 2, :]).then_inc(sq_hi_ready, 1)
                dve.wait_ge(sq_hi_ready, IC * b + m + 1)
                nc.vector.tensor_tensor(sq_lo[:, m, :], relu_sq[:, m % 2, :], sq_hi[:, m, :].bitcast(fp32),
                                        ALU.subtract).then_inc(sq_lo_ready, 1)

            def latent_low(b):
                for lc in range(LC):
                    dve.wait_ge(lat_hi_ready, LC * b + lc + 1)
                    nc.vector.tensor_tensor(lat_lo[:, lc, :], ps[:, LAT_BANK[lc], :],
                                            lat_hi[:, lc, :].bitcast(fp32), ALU.subtract).then_inc(lat_lo_ready, 1)

            def top_two(b):
                dve.wait_ge(gate_lo_ready, 1)
                dve.wait_ge(logits_done, b + 1)
                for t in range(TB):
                    nc.vector.max(out=top8[:, t, :], in_=ps[:, TOP_BANK, t * NE:(t + 1) * NE]).then_inc(top8_done, 1)
                dve.wait_ge(top8_done, TB * (b + 1))
                nc.vector.tensor_tensor(top2[:, :], top8[:, :, 0], top8[:, :, 1], ALU.add).then_inc(top2_done, 1)

            def normalise(b, t):
                n = TB * b + t + 1
                y = y_buf[:, t % 2, :]
                dve.wait_ge(scaled_done, n)
                dve.wait_ge(shared_done, n)
                nc.vector.tensor_tensor(y, shared(t), y, ALU.add).then_inc(y_done, 1)
                dve.wait_ge(y_done, n)
                nc.vector.bn_stats(out=stats[:, :], in_=y).then_inc(stats_done, 1)
                dve.wait_ge(affine_loaded, 32)
                dve.wait_ge(stats_done, n)
                nc.vector.bn_aggr(out=mv[:, :], in_=stats[:, :]).then_inc(mv_done, 1)
                dve.wait_ge(mv_done, 2 * n - 1)
                nc.vector.tensor_scalar(mv[:, 1:2], mv[:, 1:2], EPS, None, ALU.add).then_inc(mv_done, 1)
                nc.vector.scalar_tensor_tensor(out=y, in0=y, scalar=mv[:, 0:1], in1=gamma_b[:, :],
                                               op0=ALU.subtract, op1=ALU.mult).then_inc(gamma_done, 1)
                dve.wait_ge(gamma_done, n)
                dve.wait_ge(rstd_done, n)
                dve.wait_ge(xbeta_ready, b + 1)
                wait_past(dve, stored[t], 16 * b)
                nc.vector.scalar_tensor_tensor(out=out_buf[:, t, :], in0=y, scalar=rstd[:, :],
                                               in1=x_beta[:, t, :], op0=ALU.mult,
                                               op1=ALU.add).then_inc(final_done, 1)

            def down_low(i):
                ks = slice(i * DNC, (i + 1) * DNC)
                dve.wait_ge(down_hi_ready, i + 1)
                nc.vector.tensor_tensor(down_lo[:, ks, :], down_raw[:, ks, :], down_hi[:, ks, :].bitcast(fp32),
                                        ALU.subtract).then_inc(down_lo_ready, 1)

            for m in range(IC):
                split_square(0, m)
                if m % 2 == 1:
                    down_low(m // 2)
            latent_low(0)
            mix_bias(1, 0)
            mix_bias(1, 1)
            top_two(0)
            mix_low(1, 0)
            mix_bias(1, 2)
            mix_low(1, 1)
            mix_bias(1, 3)
            mix_low(1, 2)
            mix_low(1, 3)
            for t in range(TB):
                normalise(0, t)
            with dve.Fori(1, NBLK - 1) as b:
                for m in range(IC):
                    split_square(b, m)
                latent_low(b)
                mix_bias(b + 1, 0)
                mix_bias(b + 1, 1)
                top_two(b)
                mix_low(b + 1, 0)
                mix_bias(b + 1, 2)
                mix_low(b + 1, 1)
                mix_bias(b + 1, 3)
                mix_low(b + 1, 2)
                mix_low(b + 1, 3)
                for t in range(TB):
                    normalise(b, t)
            for m in range(IC):
                split_square(NBLK - 1, m)
            latent_low(NBLK - 1)
            top_two(NBLK - 1)
            for t in range(TB):
                normalise(NBLK - 1, t)

        @block.tensor
        def _(pe):
            pe.wait_ge(const_ready, 1)
            pe.wait_ge(cond_loaded, 16)
            nc.tensor.transpose(EMB, cond_in[:, :], ident[0:NB, 0:NB]).then_inc(emb_done, 1)
            pe.wait_ge(expert_loaded, 16)
            for l in range(LC):
                for m in range(LC):
                    last = nc.tensor.transpose(EXP_T[:, m, l * P:(l + 1) * P],
                                               expert_raw[:, l, m * P:(m + 1) * P], ident[:, :])
            last.then_inc(expT_done, 1)
            pe.wait_ge(emb_copied, 1)
            pe.wait_ge(w0_loaded, 32)
            nc.tensor.matmul(H1, w0_sb[:, :], cond_T[:, :], start=True, stop=True).then_inc(h1_done, 1)
            pe.wait_ge(w1_loaded, 32)
            pe.wait_ge(gelu_done, 1)
            nc.tensor.matmul(H2, w1_sb[:, :], hid1[:, :], start=True, stop=True).then_inc(h2_done, 1)
            pe.wait_ge(mix_loaded, 64)
            pe.wait_ge(dve_const, 3)
            pe.wait_ge(gelu_done, 2)
            nc.tensor.matmul(LOGIT, hid2[:, :], w2_sb[:, :], start=True, stop=False)
            nc.tensor.matmul(LOGIT, ones[0:1, 0:NB], b2_sb[:, :], start=False, stop=True).then_inc(logit_done, 1)

            def fold_expert(lc):
                for m in range(LC):
                    last = nc.tensor.matmul(Q[lc], expert_T[:, m, lc * P:(lc + 1) * P], fc2_raw[:, m, :],
                                            start=(m == 0), stop=(m == LC - 1))
                last.then_inc(q_done, 1)

            pe.wait_ge(expT_copied, 1)
            pe.wait_ge(fc2_loaded, 16)
            fold_expert(0)
            pe.wait_ge(att_done, 1)
            nc.tensor.transpose(ATT_T, att[:, :], ident[0:NB, 0:NB]).then_inc(attT_done, 1)
            pe.wait_ge(attT_copied, 1)
            for c in range(C // G):
                last = nc.tensor.matmul(AGG[:, c, :], weight_sb[:, c * P:(c + 1) * P], att_T[:, :],
                                        start=True, stop=True)
            last.then_inc(agg_done, 1)

            def sum_bias(i):
                pe.wait_ge(attb_ready, i + 1)
                nc.tensor.matmul(ps[:, AGG_B_BANK[i], :], ones[:, :], att_bias[:, i % 2, :],
                                 start=True, stop=True).then_inc(aggb_done, 1)

            def mix_chunk(b, c):
                for t in range(TB):
                    last = nc.tensor.matmul(ps[:, MIX_BANK[c], t * P:(t + 1) * P],
                                            x_cur[:, t, c * P:(c + 1) * P], mix[:, t, :], start=True, stop=True)
                last.then_inc(mix_done, 1)

            sum_bias(0)
            fold_expert(1)
            pe.wait_ge(x_loaded, 16)
            pe.wait_ge(mix0_act, 2 * G)
            pe.wait_ge(mix0_dve, 2 * G)
            mix_chunk(0, 0)
            mix_chunk(0, 1)
            mix_chunk(0, 2)
            pe.wait_ge(h_ready, 1)
            mix_chunk(0, 3)
            sum_bias(1)
            pe.wait_ge(q_lo_ready, 2)
            sum_bias(2)
            sum_bias(3)

            def three_products(dst, a_hi, a_lo, b_hi, b_lo, first, last):
                nc.tensor.matmul(dst, a_hi, b_hi, start=first, stop=False)
                nc.tensor.matmul(dst, a_hi, b_lo, start=False, stop=False)
                return nc.tensor.matmul(dst, a_lo, b_hi, start=False, stop=last)

            def up_product(b, first_block=False):
                for m in range(IC):
                    cols = slice(m * P, (m + 1) * P)
                    if first_block and m % 2 == 0:
                        pe.wait_ge(up_lo_ready, m * P // UPC + 1)
                    if m == 1:
                        wait_past(pe, top2_done, b)
                        if first_block:
                            pe.wait_ge(agg_act, 2 * G)
                            pe.wait_ge(agg_dve, 2 * G)
                    if m >= WB:
                        pe.wait_ge(relu_done, IC * b + m - WB + 1)
                    for c in range(HC):
                        if m == 0:
                            pe.wait_ge(h_hi_ready, HC * b + c + 1)
                            pe.wait_ge(h_lo_ready, HC * b + c + 1)
                        last = three_products(ps[:, UP_BANK[m], :], up_hi[:, c, cols], up_lo[:, c, cols],
                                              h_hi[:, c, :], h_lo[:, c, :], c == 0, c == HC - 1)
                    last.then_inc(up_done, 1)

            def latent_product(b):
                for lc in range(LC):
                    cols = slice(lc * P, (lc + 1) * P)
                    pe.wait_ge(relu_done, IC * b + WB + lc + 1)
                    for c in range(HC):
                        last = three_products(ps[:, LAT_BANK[lc], :], fc1_hi[:, c, cols], fc1_lo[:, c, cols],
                                              h_hi[:, c, :], h_lo[:, c, :], c == 0, c == HC - 1)
                    last.then_inc(lat_done, 1)

            def gate_product(b):
                pe.wait_ge(relu_done, IC * b + WB + LC + 1)
                for c in range(HC):
                    nc.tensor.matmul(ps[:, GATE_BANK, :], gate_hl[:, c, :], h_hi[:, c, :],
                                     start=(c == 0), stop=False)
                    last = nc.tensor.matmul(ps[:, GATE_BANK, :], gate_hl[:, c, :], h_lo[:, c, :],
                                            start=False, stop=(c == HC - 1))
                last.then_inc(gate_done, 1)

            def logits_to_rows(b):
                pe.wait_ge(lat_lo_ready, LC * b + 2)
                pe.wait_ge(gate_copied, b + 1)
                for t in range(TB):
                    last = nc.tensor.matmul(ps[:, TOP_BANK, t * NE:(t + 1) * NE],
                                            gate_sb[:, t * P:(t + 1) * P], pick[:, :],
                                            start=True, stop=True)
                last.then_inc(logits_done, 1)

            def down_product(b, first_block=False):
                for t in range(TB):
                    rows = slice(t * P, (t + 1) * P)
                    wait_past(pe, y_done, TB * b + max(t - 1, 0))
                    for lc in range(LC):
                        if t == 0:
                            pe.wait_ge(lat_hi_ready, LC * b + lc + 1)
                            pe.wait_ge(lat_lo_ready, LC * b + lc + 1)
                        last = three_products(routed(t), lat_hi[:, lc, rows], lat_lo[:, lc, rows],
                                              q_hi[:, lc, :], q_lo[:, lc, :], lc == 0, lc == LC - 1)
                    last.then_inc(routed_done, 1)
                    for m in range(IC):
                        if t == 0:
                            if first_block and m % DNC == 0:
                                pe.wait_ge(down_lo_ready, m // DNC + 1)
                            pe.wait_ge(sq_lo_ready, IC * b + m + 1)
                        last = three_products(shared(t), sq_hi[:, m, rows], sq_lo[:, m, rows],
                                              down_hi[:, m, :], down_lo[:, m, :], m == 0, m == IC - 1)
                    last.then_inc(shared_done, 1)

            def block_of(b, first_block=False, last_block=False):
                up_product(b, first_block)
                if first_block:
                    pe.wait_ge(fc1_lo_ready, 1)
                latent_product(b)
                if first_block:
                    pe.wait_ge(gate_lo_ready, 1)
                gate_product(b)
                if last_block:
                    logits_to_rows(b)
                else:
                    pe.wait_ge(x_loaded, 16 * (b + 2))
                    pe.wait_ge(mix_ready, G * (b + 1))
                    pe.wait_ge(relu_done, IC * (b + 1))
                    mix_chunk(b + 1, 0)
                    pe.wait_ge(lat_lo_ready, LC * b + 1)
                    mix_chunk(b + 1, 1)
                    logits_to_rows(b)
                    mix_chunk(b + 1, 2)
                    pe.wait_ge(h_ready, HC * (b + 1) + 1)
                    mix_chunk(b + 1, 3)
                down_product(b, first_block)

            block_of(0, first_block=True)
            with pe.Fori(1, NBLK - 1) as b:
                block_of(b)
            block_of(NBLK - 1, last_block=True)


_INS = ['x', 'cond_128', 'L0_cond_W0', 'L0_cond_b0', 'L0_cond_W1', 'L0_cond_b1', 'L0_cond_W2', 'L0_cond_b2',
        'L0_cond_weight', 'L0_cond_bias_k', 'L0_ffn_gate_w', 'L0_ffn_up_w', 'L0_ffn_down_w', 'L0_ffn_fc1_w',
        'L0_ffn_fc2_w', 'L0_ffn_expert_w', 'L0_ffn_ln_gamma', 'L0_ffn_ln_beta']
_OUTS = [((64, 32, 512), 'float32')]


def kernel(**inputs):
    import numpy as _np
    import concourse.bacc as _bacc
    from concourse import mybir as _mybir
    from concourse.bass_utils import run_bass_kernel_spmd as _run

    nc = _bacc.Bacc("TRN2", target_bir_lowering=False, num_devices=1)
    arrays, args = {}, []
    for name in _INS:
        a = _np.ascontiguousarray(inputs[name])
        arrays[f"in_{name}_dram"] = a
        args.append(nc.dram_tensor(f"in_{name}_dram", a.shape, _mybir.dt.from_np(a.dtype), kind="ExternalInput").ap())
    for i, (shape, dtype) in enumerate(_OUTS):
        dt = _mybir.dt.from_np(_np.dtype(dtype))
        args.append(nc.dram_tensor(f"out_{i}_dram", shape, dt, kind="ExternalOutput").ap())
    adaln_ffn_kernel(nc, *args)
    r = _run(nc, [arrays], core_ids=[0])
    got = tuple(r.results[0][f"out_{i}_dram"] for i in range(len(_OUTS)))
    return got[0]
```

```python
import concourse.bass as bass
from concourse import mybir
from contextlib import ExitStack


def adaln_ffn_kernel(
    nc: bass.Bass,
    x: bass.AP,
    mlp: bass.AP,
    kernels: bass.AP,
    latents: bass.AP,
    experts: bass.AP,
    up_w: bass.AP,
    down_w: bass.AP,
    affine: bass.AP,
    out: bass.AP,
):
    fp32 = mybir.dt.float32
    f32r = mybir.dt.float32r
    ALU = mybir.AluOpType
    ACT = mybir.ActivationFunctionType
    AX = mybir.AxisListType

    NB, C, HID = x.shape
    K = kernels.shape[0]
    D = mlp.shape[0]
    INT = up_w.shape[1]
    LAT = experts.shape[0]
    NE = latents.shape[1] - LAT
    P = 128
    G = P // C
    NT = NB // G
    TB = 4
    TOK = TB * P
    NBLK = NT // TB
    HC, IC, LC = HID // P, INT // P, LAT // P
    EPS = 1e-5
    GC = 96
    WB = 4
    UPC = INT // 4
    DNC = IC // 4

    UP_BANK = [m % WB for m in range(IC)]
    LAT_BANK = [0, 1]
    GATE_BANK = 2
    MIX_BANK = [3, 0, 2, 3]
    TOP_BANK = 1

    x_v = x.rearrange("(n g) c h -> (g c) n h", g=G)
    out_v = out.rearrange("(n g) c h -> (g c) n h", g=G)
    up_v = up_w.rearrange("(k p) n -> p k n", p=P)
    down_v = down_w.rearrange("(k p) n -> p k n", p=P)
    latents_v = latents.rearrange("(k p) n -> p k n", p=P)
    experts_v = experts.rearrange("(k p) n -> p k n", p=P)
    aggb_dram = nc.dram_tensor("aggb_dram", (NB * C,), fp32).ap()

    ctx = ExitStack()
    with ctx:
        def sb(name, shape, dt=fp32):
            return ctx.enter_context(nc.sbuf_tensor(name, shape, dt))

        def sem(name):
            return ctx.enter_context(nc.semaphore(name))

        up_hi = sb("up_hi", [P, HC, INT], f32r)
        up_lo = sb("up_lo", [P, HC, INT], f32r)
        down_hi = sb("down_hi", [P, IC, HID], f32r)
        down_lo = sb("down_lo", [P, IC, HID], f32r)
        fc1_hi = sb("fc1_hi", [P, HC, LAT], f32r)
        fc1_lo = sb("fc1_lo", [P, HC, LAT], f32r)
        q_hi = sb("q_hi", [P, LC, HID], f32r)
        q_lo = sb("q_lo", [P, LC, HID], f32r)
        gate_hl = sb("gate_hl", [P, HC, GC], f32r)

        h_hi = sb("h_hi", [P, HC, TOK], f32r)
        h_lo = sb("h_lo", [P, HC, TOK], f32r)
        sq_hi = sb("sq_hi", [P, IC, TOK], f32r)
        sq_lo = sb("sq_lo", [P, IC, TOK], f32r)
        lat_hi = sb("lat_hi", [P, LC, TOK], f32r)
        lat_lo = sb("lat_lo", [P, LC, TOK], f32r)
        x_cur = sb("x_cur", [P, TB, HID])
        h_full = sb("h_full", [P, 2, TOK])
        relu_sq = sb("relu_sq", [P, 2, TOK])
        y_buf = sb("y_buf", [P, 2, HID])
        late = sb("late", [P, IC * HID])
        up_raw = late[:, :].rearrange("p (k n) -> p k n", k=HC)
        down_raw = late[:, :].rearrange("p (k n) -> p k n", k=IC)
        x_beta = late[:, 0:TB * HID].rearrange("p (t n) -> p t n", t=TB)
        out_buf = late[:, TB * HID:2 * TB * HID].rearrange("p (t n) -> p t n", t=TB)
        top8 = sb("top8", [P, TB, NE])
        top2 = sb("top2", [P, TB])
        stats = sb("stats", [P, 6])
        mv = sb("mv", [P, 2])
        rstd = sb("rstd", [P, 1])

        agg = sb("agg", [P, NT, C])
        mix = sb("mix", [P, TB, P])
        agg_b = sb("agg_b", [P, NB * C])
        affine_sb = sb("affine_sb", [P, 2, HID])
        gamma_b = affine_sb[:, 0, :]
        beta_b = affine_sb[:, 1, :]

        latents_sb = sb("latents_sb", [P, HC, LAT + NE])
        fc1_raw = latents_sb[:, :, 0:LAT]
        gate_raw = latents_sb[:, :, LAT:LAT + NE]
        experts_sb = sb("experts_sb", [P, LC, LAT + HID])
        expert_T = experts_sb[:, :, 0:LAT]
        fc2_raw = experts_sb[:, :, LAT:LAT + HID]
        mlp_sb = sb("mlp_sb", [D, mlp.shape[1]])
        cond_T = mlp_sb[:, 0:NB]
        w0_sb = mlp_sb[:, NB:NB + D]
        w1_sb = mlp_sb[:, NB + D:NB + 2 * D]
        w2_sb = mlp_sb[:, NB + 2 * D:NB + 2 * D + K]
        b0_sb = mlp_sb[:, NB + 2 * D + K:NB + 2 * D + K + 1]
        b1_sb = mlp_sb[:, NB + 2 * D + K + 1:NB + 2 * D + K + 2]
        kernels_sb = sb("kernels_sb", [K, kernels.shape[1]])
        weight_sb = kernels_sb[:, 0:C * C]
        bias_sb = kernels_sb[:, C * C:C * C + C]
        b2_sb = kernels_sb[0:1, C * C + C:C * C + C + K]
        hid1 = sb("hid1", [D, NB])
        hid2 = sb("hid2", [D, NB])
        att = sb("att", [NB, K])
        att_T = sb("att_T", [K, NB])
        neg_max = sb("neg_max", [NB, 1])
        exp_sum = sb("exp_sum", [NB, 1])
        exp_inv = sb("exp_inv", [NB, 1])
        att_bias = y_buf[0:K, 0, 0:TOK]
        aggb_rows = sb("aggb_rows", [NB, C])
        gate_sb = experts_sb[0:2 * NE, 0, 0:TOK]
        ident = sb("ident", [P, P])
        pick = sb("pick", [2 * NE, NE])
        ones = sb("ones", [K, P])
        half = sb("half", [P, 1])
        warm = sb("warm", [P, 1])

        ps = ctx.enter_context(nc.psum_tensor("ps", [P, 8, TOK], fp32))
        H1 = ps[:, 4, 64:64 + NB]
        H2 = ps[:, 4, 128:128 + NB]
        LOGIT = ps[0:NB, 4, 192:192 + K]
        ATT_T = ps[0:K, 4, 256:256 + NB]
        AGG_B = ps[:, 5, :]
        AGGB_ROWS = ps[0:NB, 4, 320:320 + C]
        Q = [ps[:, 6, :], ps[:, 7, :]]
        AGG = ps[:, 1, :].rearrange("p (c b) -> p c b", b=NB)

        def agg_src(q, g, tiles):
            return AGG[q * C:(q + 1) * C, :, g:tiles * G:G]

        def agg_part(g, q):
            return agg[g * C:(g + 1) * C, :, q:C:G].rearrange("i n c -> i c n")

        def mix_part(g, q):
            return mix[g * C:(g + 1) * C, :, g * C + q:(g + 1) * C:G].rearrange("i t c -> i c t")

        def shared(t):
            return ps[:, 4 + t % 2, :]

        def routed(t):
            return ps[:, 6 + t % 2, :]

        mlp_loaded = sem("mlp_loaded")
        kernels_loaded = sem("kernels_loaded")
        experts_loaded = sem("experts_loaded")
        x_loaded = sem("x_loaded")
        up_loaded = [sem(f"up_loaded{i}") for i in range(4)]
        latents_loaded = sem("latents_loaded")
        down_loaded = [sem(f"down_loaded{i}") for i in range(4)]
        affine_loaded = sem("affine_loaded")
        stored = [sem(f"stored{t}") for t in range(TB)]
        zeroed = sem("zeroed")
        const_ready = sem("const_ready")
        dve_const = sem("dve_const")
        warmed = sem("warmed")
        h1_done = sem("h1_done")
        gelu_done = sem("gelu_done")
        h2_done = sem("h2_done")
        logit_done = sem("logit_done")
        max_done = sem("max_done")
        exp_done = sem("exp_done")
        inv_done = sem("inv_done")
        att_done = sem("att_done")
        attT_done = sem("attT_done")
        attT_copied = sem("attT_copied")
        agg_done = sem("agg_done")
        q_done = sem("q_done")
        q_hi_ready = sem("q_hi_ready")
        q_lo_ready = sem("q_lo_ready")
        attb_ready = sem("attb_ready")
        aggb_done = sem("aggb_done")
        aggb_copied = sem("aggb_copied")
        rows_done = sem("rows_done")
        rows_copied = sem("rows_copied")
        rows_stored = sem("rows_stored")
        aggb_loaded = sem("aggb_loaded")
        mix0_act = sem("mix0_act")
        mix0_dve = sem("mix0_dve")
        agg_act = sem("agg_act")
        agg_dve = sem("agg_dve")
        up_hi_ready = sem("up_hi_ready")
        up_lo_ready = sem("up_lo_ready")
        fc1_hi_ready = sem("fc1_hi_ready")
        fc1_lo_ready = sem("fc1_lo_ready")
        gate_hi_ready = sem("gate_hi_ready")
        gate_lo_ready = sem("gate_lo_ready")
        down_hi_ready = sem("down_hi_ready")
        down_lo_ready = sem("down_lo_ready")
        mix_ready = sem("mix_ready")
        mix_done = sem("mix_done")
        h_ready = sem("h_ready")
        h_hi_ready = sem("h_hi_ready")
        h_lo_ready = sem("h_lo_ready")
        up_done = sem("up_done")
        relu_done = sem("relu_done")
        square_done = sem("square_done")
        sq_hi_ready = sem("sq_hi_ready")
        sq_lo_ready = sem("sq_lo_ready")
        lat_done = sem("lat_done")
        lat_hi_ready = sem("lat_hi_ready")
        lat_lo_ready = sem("lat_lo_ready")
        gate_done = sem("gate_done")
        gate_copied = sem("gate_copied")
        logits_done = sem("logits_done")
        top8_done = sem("top8_done")
        top2_done = sem("top2_done")
        routed_done = sem("routed_done")
        scaled_done = sem("scaled_done")
        shared_done = sem("shared_done")
        y_done = sem("y_done")
        stats_done = sem("stats_done")
        mv_done = sem("mv_done")
        rstd_done = sem("rstd_done")
        gamma_done = sem("gamma_done")
        final_done = sem("final_done")
        xbeta_ready = sem("xbeta_ready")

        def wait_past(eng, semaphore, value):
            if not (isinstance(value, int) and value == 0):
                eng.wait_ge(semaphore, value)

        block = ctx.enter_context(nc.Block())

        @block.sync
        def _(sp):
            sp.dma_start(mlp_sb[:, :], mlp).then_inc(mlp_loaded, 16)
            sp.dma_start(kernels_sb[:, :], kernels).then_inc(kernels_loaded, 16)
            sp.dma_start(experts_sb[:, :, :], experts_v).then_inc(experts_loaded, 16)
            sp.dma_start(x_cur[:, :, :], x_v[:, 0:TB, :]).then_inc(x_loaded, 16)
            for i in range(4):
                sp.dma_start(up_raw[:, :, i * UPC:(i + 1) * UPC],
                             up_v[:, :, i * UPC:(i + 1) * UPC]).then_inc(up_loaded[i], 16)
            sp.wait_ge(rows_copied, 1)
            sp.dma_start(aggb_dram.rearrange("(b o) -> b o", o=C), aggb_rows[:, :]).then_inc(rows_stored, 16)
            sp.dma_start(latents_sb[:, :, :], latents_v).then_inc(latents_loaded, 16)
            sp.dma_start(affine_sb[:, :, :], affine.partition_broadcast(P)).then_inc(affine_loaded, 16)
            sp.wait_ge(rows_stored, 16)
            sp.dma_start(agg_b[:, TOK:], aggb_dram[TOK:].partition_broadcast(P)).then_inc(aggb_loaded, 16)
            sp.wait_ge(up_hi_ready, 4)
            sp.wait_ge(up_lo_ready, 4)
            for i in range(4):
                sp.dma_start(down_raw[:, i * DNC:(i + 1) * DNC, :],
                             down_v[:, i * DNC:(i + 1) * DNC, :]).then_inc(down_loaded[i], 16)

            def load_next_x(b):
                sp.wait_ge(mix_done, HC * (b + 1))
                sp.wait_ge(xbeta_ready, b + 1)
                sp.dma_start(x_cur[:, :, :], x_v[:, bass.ds((b + 1) * TB, TB), :]).then_inc(x_loaded, 16)

            def store_block(b):
                for t in range(TB):
                    sp.wait_ge(final_done, TB * b + t + 1)
                    sp.dma_start(out_v[:, bass.ds(b * TB + t, 1), :],
                                 out_buf[:, t:t + 1, :]).then_inc(stored[t], 16)

            with sp.Fori(0, NBLK - 1) as b:
                load_next_x(b)
                store_block(b)
            store_block(NBLK - 1)
            for t in range(TB):
                sp.wait_ge(stored[t], 16 * NBLK)

        @block.gpsimd
        def _(pool):
            nc.gpsimd.memset(ident[:, :], 0.0).then_inc(zeroed, 1)
            nc.gpsimd.memset(pick[:, :], 0.0).then_inc(zeroed, 1)
            pool.wait_ge(zeroed, 2)
            nc.gpsimd.affine_select(out=ident[:, :], in_=ident[:, :], compare_op=ALU.not_equal, fill=1.0,
                                    base=0, pattern=[[-1, P]], channel_multiplier=1).then_inc(const_ready, 1)
            nc.gpsimd.affine_select(out=pick[:, :], in_=pick[:, :], compare_op=ALU.not_equal, fill=1.0,
                                    base=0, pattern=[[-1, NE]], channel_multiplier=1).then_inc(zeroed, 1)
            pool.wait_ge(zeroed, 3)
            nc.gpsimd.affine_select(out=pick[:, :], in_=pick[:, :], compare_op=ALU.not_equal, fill=1.0,
                                    base=-NE, pattern=[[-1, NE]], channel_multiplier=1).then_inc(const_ready, 1)
            nc.gpsimd.memset(mix[:, :, :], 0.0).then_inc(const_ready, 1)
            nc.gpsimd.memset(half[:, :], -0.5).then_inc(const_ready, 1)
            pool.wait_ge(attT_copied, 1)
            nc.gpsimd.tensor_tensor(
                att_bias.rearrange("k (b o) -> k b o", o=C),
                att_T[:, 0:TOK // C].unsqueeze(2).to_broadcast([K, TOK // C, C]),
                bias_sb.unsqueeze(1).to_broadcast([K, TOK // C, C]), ALU.mult).then_inc(attb_ready, 1)
            pool.wait_ge(fc1_hi_ready, 1)
            nc.gpsimd.tensor_tensor(fc1_lo[:, :, :], fc1_raw, fc1_hi[:, :, :].bitcast(fp32),
                                    ALU.subtract).then_inc(fc1_lo_ready, 1)
            pool.wait_ge(gate_hi_ready, 1)
            nc.gpsimd.tensor_tensor(gate_hl[:, :, NE:2 * NE], gate_raw, gate_hl[:, :, 0:NE].bitcast(fp32),
                                    ALU.subtract).then_inc(gate_lo_ready, 1)
            pool.wait_ge(agg_act, 2 * G)
            pool.wait_ge(agg_dve, 2 * G)

            def next_mix(b):
                pool.wait_ge(mix_done, HC * (b + 1))
                pool.wait_ge(xbeta_ready, b + 1)
                for g in range(G):
                    if g > 0:
                        pool.wait_ge(mix_ready, G * b + g)
                    r = slice(g * C, (g + 1) * C)
                    nc.gpsimd.tensor_copy(mix[r, :, r], agg[r, bass.ds((b + 1) * TB, TB), :]).then_inc(mix_ready, 1)

            def x_plus_beta(b):
                pool.wait_ge(x_loaded, 16 * (b + 1))
                wait_past(pool, final_done, TB * b)
                nc.gpsimd.tensor_tensor(x_beta, x_cur[:, :, :],
                                        beta_b.unsqueeze(1).to_broadcast([P, TB, HID]),
                                        ALU.add).then_inc(xbeta_ready, 1)

            def inverse_deviations(b):
                for t in range(TB):
                    pool.wait_ge(mv_done, 2 * (TB * b + t + 1))
                    nc.gpsimd.tensor_tensor(rstd[:, :], mv[:, 1:2], half[:, :], ALU.pow).then_inc(rstd_done, 1)

            pool.wait_ge(affine_loaded, 16)
            pool.wait_ge(down_hi_ready, 2)
            pool.wait_ge(down_lo_ready, 2)
            def pool_block(b):
                x_plus_beta(b)
                next_mix(b)
                pool.wait_ge(mix_ready, G * (b + 1))
                inverse_deviations(b)

            pool_block(0)
            with pool.Fori(1, NBLK - 1) as b:
                pool_block(b)
            x_plus_beta(NBLK - 1)
            inverse_deviations(NBLK - 1)

        @block.scalar
        def _(act):
            act.wait_ge(dve_const, 1)
            nc.scalar.activation(warm[:, :], warm[:, :], ACT.Gelu).then_inc(warmed, 1)
            act.wait_ge(mlp_loaded, 16)
            act.wait_ge(h1_done, 1)
            nc.scalar.activation(hid1[:, :], H1, ACT.Gelu, bias=b0_sb).then_inc(gelu_done, 1)
            act.wait_ge(h2_done, 1)
            nc.scalar.activation(hid2[:, :], H2, ACT.Gelu, bias=b1_sb).then_inc(gelu_done, 1)
            act.wait_ge(warmed, 1)
            nc.scalar.activation(warm[:, :], warm[:, :], ACT.Exp).then_inc(warmed, 1)
            act.wait_ge(logit_done, 1)
            act.wait_ge(max_done, 1)
            nc.scalar.activation(att[:, :], LOGIT, ACT.Exp, bias=neg_max[:, :],
                                 accum_out=exp_sum[:, :]).then_inc(exp_done, 1)

            def split_up(i):
                cols = slice(i * UPC, (i + 1) * UPC)
                act.wait_ge(up_loaded[i], 16)
                nc.scalar.copy(up_hi[:, :, cols], up_raw[:, :, cols]).then_inc(up_hi_ready, 1)

            def q_high(lc):
                act.wait_ge(q_done, lc + 1)
                nc.scalar.copy(q_hi[:, lc, :], Q[lc]).then_inc(q_hi_ready, 1)

            def mix_high(b):
                for c in range(HC):
                    act.wait_ge(h_ready, HC * b + c + 1)
                    nc.scalar.copy(h_hi[:, c, :], h_full[:, c % 2, :]).then_inc(h_hi_ready, 1)

            act.wait_ge(const_ready, 3)
            act.wait_ge(agg_done, 1)
            for q in (0, 1):
                for g in range(G):
                    nc.scalar.copy(mix_part(g, q), agg_src(q, g, TB)).then_inc(mix0_act, 1)
            act.wait_ge(aggb_done, 1)
            nc.scalar.copy(agg_b[:, 0:TOK], AGG_B).then_inc(aggb_copied, 1)
            split_up(0)
            mix_high(0)
            act.wait_ge(rows_done, 1)
            nc.scalar.copy(aggb_rows[:, :], AGGB_ROWS).then_inc(rows_copied, 1)
            split_up(1)
            split_up(2)
            split_up(3)
            for q in (0, 1):
                for g in range(G):
                    nc.scalar.copy(agg_part(g, q), agg_src(q, g, NT)).then_inc(agg_act, 1)
            act.wait_ge(latents_loaded, 16)
            nc.scalar.copy(fc1_hi[:, :, :], fc1_raw).then_inc(fc1_hi_ready, 1)
            act.wait_ge(dve_const, 2)
            nc.scalar.copy(gate_hl[:, :, 0:NE], gate_raw).then_inc(gate_hi_ready, 1)

            def relu_square(b, m):
                act.wait_ge(up_done, IC * b + m + 1)
                wait_past(act, sq_lo_ready, IC * b + max(m - 1, 0))
                nc.scalar.activation(relu_sq[:, m % 2, :], ps[:, UP_BANK[m], :], ACT.Relu).then_inc(relu_done, 1)
                act.wait_ge(relu_done, IC * b + m + 1)
                nc.scalar.activation(relu_sq[:, m % 2, :], relu_sq[:, m % 2, :], ACT.Square).then_inc(square_done, 1)

            def latent_gate(b):
                for lc in range(LC):
                    act.wait_ge(lat_done, LC * b + lc + 1)
                    nc.scalar.copy(lat_hi[:, lc, :], ps[:, LAT_BANK[lc], :]).then_inc(lat_hi_ready, 1)
                act.wait_ge(gate_done, b + 1)
                nc.scalar.copy(gate_sb, ps[0:2 * NE, GATE_BANK, :]).then_inc(gate_copied, 1)

            def scale_routed(b):
                act.wait_ge(top2_done, b + 1)
                for t in range(TB):
                    act.wait_ge(routed_done, TB * b + t + 1)
                    wait_past(act, final_done, TB * b + max(t - 1, 0))
                    nc.scalar.mul(y_buf[:, t % 2, :], routed(t), top2[:, t:t + 1]).then_inc(scaled_done, 1)

            def down_high(i):
                ks = slice(i * DNC, (i + 1) * DNC)
                act.wait_ge(down_loaded[i], 16)
                nc.scalar.copy(down_hi[:, ks, :], down_raw[:, ks, :]).then_inc(down_hi_ready, 1)

            for m in range(IC):
                relu_square(0, m)
                if m in (0, 1):
                    q_high(m)
                if m in (2, 3, 4, 5):
                    down_high(m - 2)
            latent_gate(0)
            mix_high(1)
            scale_routed(0)
            with act.Fori(1, NBLK - 1) as b:
                for m in range(IC):
                    relu_square(b, m)
                latent_gate(b)
                mix_high(b + 1)
                scale_routed(b)
            for m in range(IC):
                relu_square(NBLK - 1, m)
            latent_gate(NBLK - 1)
            scale_routed(NBLK - 1)

        @block.vector
        def _(dve):
            nc.vector.memset(warm[:, :], 0.0).then_inc(dve_const, 1)
            nc.vector.memset(gate_hl[:, :, :].bitcast(mybir.dt.uint32), 0).then_inc(dve_const, 1)
            nc.vector.memset(ones[:, :], 1.0).then_inc(dve_const, 1)
            dve.wait_ge(logit_done, 1)
            nc.vector.tensor_reduce(neg_max[:, :], LOGIT, AX.X, ALU.max, negate=True).then_inc(max_done, 1)
            dve.wait_ge(exp_done, 1)
            nc.vector.reciprocal(exp_inv[:, :], exp_sum[:, :]).then_inc(inv_done, 1)
            dve.wait_ge(inv_done, 1)
            nc.vector.tensor_scalar(att[:, :], att[:, :], exp_inv[:, :], None, ALU.mult).then_inc(att_done, 1)
            dve.wait_ge(attT_done, 1)
            nc.vector.tensor_copy(att_T[:, :], ATT_T).then_inc(attT_copied, 1)

            def split_up(i):
                cols = slice(i * UPC, (i + 1) * UPC)
                dve.wait_ge(up_hi_ready, i + 1)
                nc.vector.tensor_tensor(up_lo[:, :, cols], up_raw[:, :, cols],
                                        up_hi[:, :, cols].bitcast(fp32), ALU.subtract).then_inc(up_lo_ready, 1)

            def q_low(lc):
                dve.wait_ge(q_hi_ready, lc + 1)
                nc.vector.tensor_tensor(q_lo[:, lc, :], Q[lc], q_hi[:, lc, :].bitcast(fp32),
                                        ALU.subtract).then_inc(q_lo_ready, 1)

            def mix_bias(b, c):
                dve.wait_ge(mix_done, HC * b + c + 1)
                wait_past(dve, h_hi_ready, HC * b + max(c - 1, 0))
                wait_past(dve, h_lo_ready, HC * b + max(c - 1, 0))
                nc.vector.tensor_tensor(h_full[:, c % 2, :], ps[:, MIX_BANK[c], :],
                                        agg_b[:, bass.ds(b * TOK, TOK)], ALU.add).then_inc(h_ready, 1)

            def mix_low(b, c):
                dve.wait_ge(h_hi_ready, HC * b + c + 1)
                nc.vector.tensor_tensor(h_lo[:, c, :], h_full[:, c % 2, :], h_hi[:, c, :].bitcast(fp32),
                                        ALU.subtract).then_inc(h_lo_ready, 1)

            dve.wait_ge(const_ready, 3)
            dve.wait_ge(agg_done, 1)
            for q in (2, 3):
                for g in range(G):
                    nc.vector.tensor_copy(mix_part(g, q), agg_src(q, g, TB)).then_inc(mix0_dve, 1)
            dve.wait_ge(aggb_copied, 1)
            mix_bias(0, 0)
            mix_bias(0, 1)
            split_up(0)
            mix_low(0, 0)
            mix_bias(0, 2)
            mix_low(0, 1)
            mix_bias(0, 3)
            mix_low(0, 2)
            mix_low(0, 3)
            split_up(1)
            split_up(2)
            split_up(3)
            for q in (2, 3):
                for g in range(G):
                    nc.vector.tensor_copy(agg_part(g, q), agg_src(q, g, NT)).then_inc(agg_dve, 1)
            def split_square(b, m):
                dve.wait_ge(square_done, IC * b + m + 1)
                nc.vector.tensor_copy(sq_hi[:, m, :], relu_sq[:, m % 2, :]).then_inc(sq_hi_ready, 1)
                dve.wait_ge(sq_hi_ready, IC * b + m + 1)
                nc.vector.tensor_tensor(sq_lo[:, m, :], relu_sq[:, m % 2, :], sq_hi[:, m, :].bitcast(fp32),
                                        ALU.subtract).then_inc(sq_lo_ready, 1)

            def latent_low(b):
                for lc in range(LC):
                    dve.wait_ge(lat_hi_ready, LC * b + lc + 1)
                    nc.vector.tensor_tensor(lat_lo[:, lc, :], ps[:, LAT_BANK[lc], :],
                                            lat_hi[:, lc, :].bitcast(fp32), ALU.subtract).then_inc(lat_lo_ready, 1)

            def top_two(b):
                dve.wait_ge(gate_lo_ready, 1)
                dve.wait_ge(logits_done, b + 1)
                for t in range(TB):
                    nc.vector.max(out=top8[:, t, :], in_=ps[:, TOP_BANK, t * NE:(t + 1) * NE]).then_inc(top8_done, 1)
                dve.wait_ge(top8_done, TB * (b + 1))
                nc.vector.tensor_tensor(top2[:, :], top8[:, :, 0], top8[:, :, 1], ALU.add).then_inc(top2_done, 1)

            def normalise(b, t):
                n = TB * b + t + 1
                y = y_buf[:, t % 2, :]
                dve.wait_ge(scaled_done, n)
                dve.wait_ge(shared_done, n)
                nc.vector.tensor_tensor(y, shared(t), y, ALU.add).then_inc(y_done, 1)
                dve.wait_ge(y_done, n)
                nc.vector.bn_stats(out=stats[:, :], in_=y).then_inc(stats_done, 1)
                dve.wait_ge(affine_loaded, 16)
                dve.wait_ge(stats_done, n)
                nc.vector.bn_aggr(out=mv[:, :], in_=stats[:, :]).then_inc(mv_done, 1)
                dve.wait_ge(mv_done, 2 * n - 1)
                nc.vector.tensor_scalar(mv[:, 1:2], mv[:, 1:2], EPS, None, ALU.add).then_inc(mv_done, 1)
                nc.vector.scalar_tensor_tensor(out=y, in0=y, scalar=mv[:, 0:1], in1=gamma_b,
                                               op0=ALU.subtract, op1=ALU.mult).then_inc(gamma_done, 1)
                dve.wait_ge(gamma_done, n)
                dve.wait_ge(rstd_done, n)
                dve.wait_ge(xbeta_ready, b + 1)
                wait_past(dve, stored[t], 16 * b)
                nc.vector.scalar_tensor_tensor(out=out_buf[:, t, :], in0=y, scalar=rstd[:, :],
                                               in1=x_beta[:, t, :], op0=ALU.mult,
                                               op1=ALU.add).then_inc(final_done, 1)

            def down_low(i):
                ks = slice(i * DNC, (i + 1) * DNC)
                dve.wait_ge(down_hi_ready, i + 1)
                nc.vector.tensor_tensor(down_lo[:, ks, :], down_raw[:, ks, :], down_hi[:, ks, :].bitcast(fp32),
                                        ALU.subtract).then_inc(down_lo_ready, 1)

            for m in range(IC):
                split_square(0, m)
                if m in (0, 1):
                    q_low(m)
                if m in (2, 3, 4, 5):
                    down_low(m - 2)
            latent_low(0)
            dve.wait_ge(aggb_loaded, 16)
            mix_bias(1, 0)
            mix_bias(1, 1)
            top_two(0)
            mix_low(1, 0)
            mix_bias(1, 2)
            mix_low(1, 1)
            mix_bias(1, 3)
            mix_low(1, 2)
            mix_low(1, 3)
            for t in range(TB):
                normalise(0, t)
            with dve.Fori(1, NBLK - 1) as b:
                for m in range(IC):
                    split_square(b, m)
                latent_low(b)
                mix_bias(b + 1, 0)
                mix_bias(b + 1, 1)
                top_two(b)
                mix_low(b + 1, 0)
                mix_bias(b + 1, 2)
                mix_low(b + 1, 1)
                mix_bias(b + 1, 3)
                mix_low(b + 1, 2)
                mix_low(b + 1, 3)
                for t in range(TB):
                    normalise(b, t)
            for m in range(IC):
                split_square(NBLK - 1, m)
            latent_low(NBLK - 1)
            top_two(NBLK - 1)
            for t in range(TB):
                normalise(NBLK - 1, t)

        @block.tensor
        def _(pe):
            pe.wait_ge(mlp_loaded, 16)
            nc.tensor.matmul(H1, w0_sb, cond_T, start=True, stop=True).then_inc(h1_done, 1)
            pe.wait_ge(gelu_done, 1)
            nc.tensor.matmul(H2, w1_sb, hid1[:, :], start=True, stop=True).then_inc(h2_done, 1)
            pe.wait_ge(kernels_loaded, 16)
            pe.wait_ge(dve_const, 3)
            pe.wait_ge(gelu_done, 2)
            nc.tensor.matmul(LOGIT, hid2[:, :], w2_sb, start=True, stop=False)
            nc.tensor.matmul(LOGIT, ones[0:1, 0:NB], b2_sb, start=False, stop=True).then_inc(logit_done, 1)

            def fold_expert(lc):
                for m in range(LC):
                    last = nc.tensor.matmul(Q[lc], expert_T[:, m, lc * P:(lc + 1) * P], fc2_raw[:, m, :],
                                            start=(m == 0), stop=(m == LC - 1))
                last.then_inc(q_done, 1)

            pe.wait_ge(const_ready, 1)
            pe.wait_ge(att_done, 1)
            nc.tensor.transpose(ATT_T, att[:, :], ident[0:NB, 0:NB]).then_inc(attT_done, 1)
            pe.wait_ge(attT_copied, 1)
            for c in range(C // G):
                last = nc.tensor.matmul(AGG[:, c, :], weight_sb[:, c * P:(c + 1) * P], att_T[:, :],
                                        start=True, stop=True)
            last.then_inc(agg_done, 1)

            pe.wait_ge(attb_ready, 1)
            nc.tensor.matmul(AGG_B, ones[:, :], att_bias, start=True, stop=True).then_inc(aggb_done, 1)
            nc.tensor.matmul(AGGB_ROWS, att_T[:, :], bias_sb, start=True, stop=True).then_inc(rows_done, 1)

            def mix_chunk(b, c):
                for t in range(TB):
                    last = nc.tensor.matmul(ps[:, MIX_BANK[c], t * P:(t + 1) * P],
                                            x_cur[:, t, c * P:(c + 1) * P], mix[:, t, :], start=True, stop=True)
                last.then_inc(mix_done, 1)

            pe.wait_ge(x_loaded, 16)
            pe.wait_ge(mix0_act, 2 * G)
            pe.wait_ge(mix0_dve, 2 * G)
            mix_chunk(0, 0)
            mix_chunk(0, 1)
            mix_chunk(0, 2)
            pe.wait_ge(h_ready, 1)
            mix_chunk(0, 3)
            pe.wait_ge(experts_loaded, 16)
            fold_expert(0)
            fold_expert(1)

            def three_products(dst, a_hi, a_lo, b_hi, b_lo, first, last):
                nc.tensor.matmul(dst, a_hi, b_hi, start=first, stop=False)
                nc.tensor.matmul(dst, a_hi, b_lo, start=False, stop=False)
                return nc.tensor.matmul(dst, a_lo, b_hi, start=False, stop=last)

            def up_product(b, first_block=False):
                for m in range(IC):
                    cols = slice(m * P, (m + 1) * P)
                    if first_block and m % 2 == 0:
                        pe.wait_ge(up_lo_ready, m * P // UPC + 1)
                    if m == 1:
                        wait_past(pe, top2_done, b)
                        if first_block:
                            pe.wait_ge(agg_act, 2 * G)
                            pe.wait_ge(agg_dve, 2 * G)
                    if m >= WB:
                        pe.wait_ge(relu_done, IC * b + m - WB + 1)
                    for c in range(HC):
                        if m == 0:
                            pe.wait_ge(h_hi_ready, HC * b + c + 1)
                            pe.wait_ge(h_lo_ready, HC * b + c + 1)
                        last = three_products(ps[:, UP_BANK[m], :], up_hi[:, c, cols], up_lo[:, c, cols],
                                              h_hi[:, c, :], h_lo[:, c, :], c == 0, c == HC - 1)
                    last.then_inc(up_done, 1)

            def latent_product(b):
                for lc in range(LC):
                    cols = slice(lc * P, (lc + 1) * P)
                    pe.wait_ge(relu_done, IC * b + WB + lc + 1)
                    for c in range(HC):
                        last = three_products(ps[:, LAT_BANK[lc], :], fc1_hi[:, c, cols], fc1_lo[:, c, cols],
                                              h_hi[:, c, :], h_lo[:, c, :], c == 0, c == HC - 1)
                    last.then_inc(lat_done, 1)

            def gate_product(b):
                pe.wait_ge(relu_done, IC * b + WB + LC + 1)
                for c in range(HC):
                    nc.tensor.matmul(ps[0:GC, GATE_BANK, :], gate_hl[:, c, :], h_hi[:, c, :],
                                     start=(c == 0), stop=False)
                    last = nc.tensor.matmul(ps[0:GC, GATE_BANK, :], gate_hl[:, c, :], h_lo[:, c, :],
                                            start=False, stop=(c == HC - 1))
                last.then_inc(gate_done, 1)

            def logits_to_rows(b):
                pe.wait_ge(lat_lo_ready, LC * b + 2)
                pe.wait_ge(gate_copied, b + 1)
                for t in range(TB):
                    last = nc.tensor.matmul(ps[:, TOP_BANK, t * NE:(t + 1) * NE],
                                            gate_sb[:, t * P:(t + 1) * P], pick[:, :],
                                            start=True, stop=True)
                last.then_inc(logits_done, 1)

            def down_product(b, first_block=False):
                for t in range(TB):
                    rows = slice(t * P, (t + 1) * P)
                    wait_past(pe, y_done, TB * b + max(t - 1, 0))
                    for lc in range(LC):
                        if t == 0:
                            pe.wait_ge(lat_hi_ready, LC * b + lc + 1)
                            pe.wait_ge(lat_lo_ready, LC * b + lc + 1)
                        last = three_products(routed(t), lat_hi[:, lc, rows], lat_lo[:, lc, rows],
                                              q_hi[:, lc, :], q_lo[:, lc, :], lc == 0, lc == LC - 1)
                    last.then_inc(routed_done, 1)
                    for m in range(IC):
                        if t == 0:
                            if first_block and m % DNC == 0:
                                pe.wait_ge(down_lo_ready, m // DNC + 1)
                            pe.wait_ge(sq_lo_ready, IC * b + m + 1)
                        last = three_products(shared(t), sq_hi[:, m, rows], sq_lo[:, m, rows],
                                              down_hi[:, m, :], down_lo[:, m, :], m == 0, m == IC - 1)
                    last.then_inc(shared_done, 1)

            def block_of(b, first_block=False, last_block=False):
                up_product(b, first_block)
                if first_block:
                    pe.wait_ge(fc1_lo_ready, 1)
                latent_product(b)
                if first_block:
                    pe.wait_ge(gate_lo_ready, 1)
                gate_product(b)
                if last_block:
                    logits_to_rows(b)
                else:
                    pe.wait_ge(x_loaded, 16 * (b + 2))
                    pe.wait_ge(mix_ready, G * (b + 1))
                    pe.wait_ge(relu_done, IC * (b + 1))
                    mix_chunk(b + 1, 0)
                    pe.wait_ge(lat_lo_ready, LC * b + 1)
                    mix_chunk(b + 1, 1)
                    logits_to_rows(b)
                    mix_chunk(b + 1, 2)
                    pe.wait_ge(h_ready, HC * (b + 1) + 1)
                    mix_chunk(b + 1, 3)
                down_product(b, first_block)

            block_of(0, first_block=True)
            with pe.Fori(1, NBLK - 1) as b:
                block_of(b)
            block_of(NBLK - 1, last_block=True)


_OUTS = [((64, 32, 512), 'float32')]


def kernel(x, cond_128, L0_cond_W0, L0_cond_b0, L0_cond_W1, L0_cond_b1, L0_cond_W2, L0_cond_b2, L0_cond_weight,
           L0_cond_bias_k, L0_ffn_gate_w, L0_ffn_up_w, L0_ffn_down_w, L0_ffn_fc1_w, L0_ffn_fc2_w,
           L0_ffn_expert_w, L0_ffn_ln_gamma, L0_ffn_ln_beta):
    import numpy as _np
    import concourse.bacc as _bacc
    from concourse import mybir as _mybir
    from concourse.bass_utils import run_bass_kernel_spmd as _run

    a = [_np.asarray(v) for v in (cond_128, L0_cond_W0, L0_cond_W1, L0_cond_W2, L0_cond_b0, L0_cond_b1)]
    cond, w0, w1, w2, b0, b1 = a
    weight, bias_k, b2 = (_np.asarray(v) for v in (L0_cond_weight, L0_cond_bias_k, L0_cond_b2))
    nk = bias_k.shape[0]
    b2_rows = _np.zeros((nk, nk), b2.dtype)
    b2_rows[0] = b2
    ins = {
        "x": x,
        "mlp": _np.concatenate([cond.T, w0, w1, w2, b0[:, None], b1[:, None]], axis=1),
        "kernels": _np.concatenate([weight.reshape(nk, -1), bias_k, b2_rows], axis=1),
        "latents": _np.concatenate([_np.asarray(L0_ffn_fc1_w), _np.asarray(L0_ffn_gate_w)], axis=1),
        "experts": _np.concatenate([_np.asarray(L0_ffn_expert_w).T, _np.asarray(L0_ffn_fc2_w)], axis=1),
        "up_w": L0_ffn_up_w,
        "down_w": L0_ffn_down_w,
        "affine": _np.stack([_np.asarray(L0_ffn_ln_gamma), _np.asarray(L0_ffn_ln_beta)]),
    }
    nc = _bacc.Bacc("TRN2", target_bir_lowering=False, num_devices=1)
    arrays, args = {}, []
    for name, value in ins.items():
        v = _np.ascontiguousarray(value)
        arrays[f"in_{name}_dram"] = v
        args.append(nc.dram_tensor(f"in_{name}_dram", v.shape, _mybir.dt.from_np(v.dtype), kind="ExternalInput").ap())
    for i, (shape, dtype) in enumerate(_OUTS):
        dt = _mybir.dt.from_np(_np.dtype(dtype))
        args.append(nc.dram_tensor(f"out_{i}_dram", shape, dt, kind="ExternalOutput").ap())
    adaln_ffn_kernel(nc, *args)
    r = _run(nc, [arrays], core_ids=[0])
    got = tuple(r.results[0][f"out_{i}_dram"] for i in range(len(_OUTS)))
    return got[0]
```

```python
import concourse.bass as bass
from concourse import mybir
from contextlib import ExitStack


def adaln_ffn_kernel(
    nc: bass.Bass,
    x: bass.AP,
    mlp: bass.AP,
    kernels: bass.AP,
    latents: bass.AP,
    experts: bass.AP,
    up_w: bass.AP,
    down_w: bass.AP,
    affine: bass.AP,
    out: bass.AP,
):
    fp32 = mybir.dt.float32
    f32r = mybir.dt.float32r
    ALU = mybir.AluOpType
    ACT = mybir.ActivationFunctionType
    AX = mybir.AxisListType

    NB, C, HID = x.shape
    D = mlp.shape[0]
    K = mlp.shape[1] - NB - 2 * D - 2
    SR = kernels.shape[0]
    FIRST, LAST = slice(0, K), slice(SR - K, SR)
    INT = up_w.shape[1]
    LAT = experts.shape[0]
    NE = latents.shape[1] - LAT
    P = 128
    G = P // C
    NT = NB // G
    TB = 4
    TOK = TB * P
    NBLK = NT // TB
    HC, IC, LC = HID // P, INT // P, LAT // P
    EPS = 1e-5
    ONE_BITS = 0x3F800000
    GC = 96
    WB = 4
    UPC = INT // 4
    DNC = IC // 4

    UP_BANK = [m % WB for m in range(IC)]
    LAT_BANK = [0, 1]
    GATE_BANK = 2
    MIX_BANK = [3, 0, 2, 3]
    MIX0_BANK = [7, 4, 7, 4]
    TOP_BANK = 1

    x_v = x.rearrange("(n g) c h -> (g c) n h", g=G)
    out_v = out.rearrange("(n g) c h -> (g c) n h", g=G)
    up_v = up_w.rearrange("(k p) n -> p k n", p=P)
    down_v = down_w.rearrange("(k p) n -> p k n", p=P)
    latents_v = latents.rearrange("(k p) n -> p k n", p=P)
    experts_v = experts.rearrange("(k p) n -> p k n", p=P)
    aggb_dram = nc.dram_tensor("aggb_dram", (NB * C,), fp32).ap()

    ctx = ExitStack()
    with ctx:
        def sb(name, shape, dt=fp32):
            return ctx.enter_context(nc.sbuf_tensor(name, shape, dt))

        def sem(name):
            return ctx.enter_context(nc.semaphore(name))

        up_hi = sb("up_hi", [P, HC, INT], f32r)
        up_lo = sb("up_lo", [P, HC, INT], f32r)
        down_hi = sb("down_hi", [P, IC, HID], f32r)
        down_lo = sb("down_lo", [P, IC, HID], f32r)
        fc1_hi = sb("fc1_hi", [P, HC, LAT], f32r)
        fc1_lo = sb("fc1_lo", [P, HC, LAT], f32r)
        q_hi = sb("q_hi", [P, LC, HID], f32r)
        q_lo = sb("q_lo", [P, LC, HID], f32r)
        gate_hl = sb("gate_hl", [P, HC, GC], f32r)

        h_hi = sb("h_hi", [P, HC, TOK], f32r)
        h_lo = sb("h_lo", [P, HC, TOK], f32r)
        sq_hi = sb("sq_hi", [P, IC, TOK], f32r)
        sq_lo = sb("sq_lo", [P, IC, TOK], f32r)
        lat_hi = sb("lat_hi", [P, LC, TOK], f32r)
        lat_lo = sb("lat_lo", [P, LC, TOK], f32r)
        x_cur = sb("x_cur", [P, TB, HID])
        h_full = sb("h_full", [P, 2, TOK])
        relu_sq = sb("relu_sq", [P, 2, TOK])
        y_buf = sb("y_buf", [P, 2, HID])
        late = sb("late", [P, IC * HID])
        up_raw = late[:, :].rearrange("p (k n) -> p k n", k=HC)
        down_raw = late[:, :].rearrange("p (k n) -> p k n", k=IC)
        x_beta = late[:, 0:TB * HID].rearrange("p (t n) -> p t n", t=TB)
        out_buf = late[:, TB * HID:2 * TB * HID].rearrange("p (t n) -> p t n", t=TB)
        top8 = sb("top8", [P, TB, NE])
        top2 = sb("top2", [P, TB])
        stats = sb("stats", [P, 6])
        last_stats = sb("last_stats", [P, 2, 6])
        mv = sb("mv", [P, 2])
        rstd = sb("rstd", [P, 1])

        agg = sb("agg", [P, NT, C])
        mix = sb("mix", [P, TB, P])
        agg_b = sb("agg_b", [P, NB * C])
        affine_sb = sb("affine_sb", [P, 2, HID])
        gamma_b = affine_sb[:, 0, :]
        beta_b = affine_sb[:, 1, :]

        latents_sb = sb("latents_sb", [P, HC, LAT + NE])
        fc1_raw = latents_sb[:, :, 0:LAT]
        gate_raw = latents_sb[:, :, LAT:LAT + NE]
        experts_sb = sb("experts_sb", [P, LC, LAT + HID])
        expert_T = experts_sb[:, :, 0:LAT]
        fc2_raw = experts_sb[:, :, LAT:LAT + HID]
        mlp_sb = sb("mlp_sb", [D, mlp.shape[1]])
        cond_T = mlp_sb[:, 0:NB]
        w0_sb = mlp_sb[:, NB:NB + D]
        w1_sb = mlp_sb[:, NB + D:NB + 2 * D]
        w2_sb = mlp_sb[:, NB + 2 * D:NB + 2 * D + K]
        b0_sb = mlp_sb[:, NB + 2 * D + K:NB + 2 * D + K + 1]
        b1_sb = mlp_sb[:, NB + 2 * D + K + 1:NB + 2 * D + K + 2]
        kernels_sb = sb("kernels_sb", [SR, kernels.shape[1]])
        weight_raw = kernels_sb[:, 0:C * C]
        bias_raw = kernels_sb[:, C * C:C * C + C]
        b2_sb = kernels_sb[0:1, C * C + C:C * C + C + K]
        hid1 = sb("hid1", [D, NB])
        hid2 = sb("hid2", [D, NB])
        att_exp = sb("att_exp", [NB, K])
        att = relu_sq[0:NB, 0, 0:SR]
        att_T = relu_sq[0:2 * K, 1, 0:NB]
        att_parts = sq_hi[0:SR, C * C // TOK, 0:NB]
        weight_parts = sq_hi[0:SR, 0:C * C // TOK, :].rearrange("k a n -> k (a n)")
        bias_parts = sq_lo[0:2 * K, 0, :]
        neg_max = sb("neg_max", [NB, 1])
        exp_sum = sb("exp_sum", [NB, 1])
        exp_inv = sb("exp_inv", [NB, 1])
        att_bias = y_buf[0:2 * K, 0, 0:TOK]
        aggb_rows = sb("aggb_rows", [NB, C])
        gate_sb = experts_sb[0:2 * NE, 0, 0:TOK]
        ident = sb("ident", [P, P])
        logits = sb("logits", [P, TB, NE])
        ones = sq_lo[0:2 * K, 1, 0:P]
        half = sb("half", [P, 1])
        warm = sb("warm", [P, 1])

        ps = ctx.enter_context(nc.psum_tensor("ps", [P, 8, TOK], fp32))
        H1 = ps[:, 4, 64:64 + NB]
        H2 = ps[:, 4, 128:128 + NB]
        LOGIT = ps[0:NB, 4, 192:192 + K]
        ATT_T = ps[0:SR, 4, 256:256 + NB]
        IDLE = ps[0:GC, 0, 0:2 * GC]
        AGG_B = ps[:, 1, :]
        AGGB_ROWS = ps[0:NB, 3, 0:C]
        TOP = ps[:, TOP_BANK, 0:TB * 2 * NE].rearrange("p (t s n) -> p t n s", t=TB, s=2)
        Q = [ps[:, 6, :], ps[:, 7, :]]
        AGG = ps[:, 5, :].rearrange("p (c b) -> p c b", b=NB)

        def agg_src(q, g, tiles):
            return AGG[q * C:(q + 1) * C, :, g:tiles * G:G]

        def agg_part(g, q):
            return agg[g * C:(g + 1) * C, :, q:C:G].rearrange("i n c -> i c n")

        def mix_part(g, q):
            return mix[g * C:(g + 1) * C, :, g * C + q:(g + 1) * C:G].rearrange("i t c -> i c t")

        def shared(t):
            return ps[:, 4 + t % 2, :]

        def routed(t):
            return ps[:, 6 + t % 2, :]

        def last_shared(half):
            return [shared(TB - 1), ps[:, LAT_BANK[0], :]][half][:, 0:HID // 2]

        mlp_loaded = sem("mlp_loaded")
        kernels_loaded = sem("kernels_loaded")
        experts_loaded = sem("experts_loaded")
        x_loaded = sem("x_loaded")
        up_loaded = [sem(f"up_loaded{i}") for i in range(4)]
        latents_loaded = sem("latents_loaded")
        down_loaded = [sem(f"down_loaded{i}") for i in range(4)]
        affine_loaded = sem("affine_loaded")
        stored = [sem(f"stored{t}") for t in range(TB)]
        zeroed = sem("zeroed")
        const_ready = sem("const_ready")
        dve_const = sem("dve_const")
        warmed = sem("warmed")
        h1_done = sem("h1_done")
        gelu_done = sem("gelu_done")
        h2_done = sem("h2_done")
        logit_done = sem("logit_done")
        max_done = sem("max_done")
        exp_done = sem("exp_done")
        inv_done = sem("inv_done")
        att_done = sem("att_done")
        attT_done = sem("attT_done")
        attT_copied = sem("attT_copied")
        att_hi_ready = sem("att_hi_ready")
        att_lo_ready = sem("att_lo_ready")
        weight_hi_ready = sem("weight_hi_ready")
        weight_lo_ready = sem("weight_lo_ready")
        attb_hi_ready = sem("attb_hi_ready")
        attb_lo_ready = sem("attb_lo_ready")
        agg_done = sem("agg_done")
        q_done = sem("q_done")
        q_hi_ready = sem("q_hi_ready")
        q_lo_ready = sem("q_lo_ready")
        attb_ready = sem("attb_ready")
        aggb_done = sem("aggb_done")
        aggb_copied = sem("aggb_copied")
        rows_done = sem("rows_done")
        rows_copied = sem("rows_copied")
        rows_stored = sem("rows_stored")
        aggb_loaded = sem("aggb_loaded")
        mix0_act = sem("mix0_act")
        mix0_dve = sem("mix0_dve")
        agg_act = sem("agg_act")
        agg_dve = sem("agg_dve")
        up_hi_ready = sem("up_hi_ready")
        up_lo_ready = sem("up_lo_ready")
        fc1_hi_ready = sem("fc1_hi_ready")
        fc1_lo_ready = sem("fc1_lo_ready")
        gate_hi_ready = sem("gate_hi_ready")
        gate_lo_ready = sem("gate_lo_ready")
        down_hi_ready = sem("down_hi_ready")
        down_lo_ready = sem("down_lo_ready")
        mix_ready = sem("mix_ready")
        mix_done = sem("mix_done")
        h_ready = sem("h_ready")
        h_hi_ready = sem("h_hi_ready")
        h_lo_ready = sem("h_lo_ready")
        up_done = sem("up_done")
        relu_done = sem("relu_done")
        square_done = sem("square_done")
        sq_hi_ready = sem("sq_hi_ready")
        sq_lo_ready = sem("sq_lo_ready")
        lat_done = sem("lat_done")
        lat_hi_ready = sem("lat_hi_ready")
        lat_lo_ready = sem("lat_lo_ready")
        gate_done = sem("gate_done")
        gate_copied = sem("gate_copied")
        logits_done = sem("logits_done")
        logits_summed = sem("logits_summed")
        top8_done = sem("top8_done")
        top2_done = sem("top2_done")
        routed_done = sem("routed_done")
        scaled_done = sem("scaled_done")
        shared_done = sem("shared_done")
        y_done = sem("y_done")
        stats_done = sem("stats_done")
        mv_done = sem("mv_done")
        rstd_done = sem("rstd_done")
        gamma_done = sem("gamma_done")
        final_done = sem("final_done")
        xbeta_ready = sem("xbeta_ready")

        def wait_past(eng, semaphore, value):
            if not (isinstance(value, int) and value == 0):
                eng.wait_ge(semaphore, value)

        block = ctx.enter_context(nc.Block())

        @block.sync
        def _(sp):
            sp.dma_start(mlp_sb[:, :], mlp).then_inc(mlp_loaded, 16)
            sp.dma_start(kernels_sb[:, :], kernels).then_inc(kernels_loaded, 16)
            sp.dma_start(experts_sb[:, :, :], experts_v).then_inc(experts_loaded, 16)
            sp.dma_start(x_cur[:, :, :], x_v[:, 0:TB, :]).then_inc(x_loaded, 16)
            for i in range(4):
                sp.dma_start(up_raw[:, :, i * UPC:(i + 1) * UPC],
                             up_v[:, :, i * UPC:(i + 1) * UPC]).then_inc(up_loaded[i], 16)
            sp.wait_ge(rows_copied, 1)
            sp.dma_start(aggb_dram.rearrange("(b o) -> b o", o=C), aggb_rows[:, :]).then_inc(rows_stored, 16)
            sp.dma_start(latents_sb[:, :, :], latents_v).then_inc(latents_loaded, 16)
            sp.dma_start(affine_sb[:, :, :], affine.partition_broadcast(P)).then_inc(affine_loaded, 16)
            sp.wait_ge(rows_stored, 16)
            sp.dma_start(agg_b[:, TOK:], aggb_dram[TOK:].partition_broadcast(P)).then_inc(aggb_loaded, 16)
            sp.wait_ge(up_hi_ready, 4)
            sp.wait_ge(up_lo_ready, IC)
            for i in range(4):
                sp.dma_start(down_raw[:, i * DNC:(i + 1) * DNC, :],
                             down_v[:, i * DNC:(i + 1) * DNC, :]).then_inc(down_loaded[i], 16)

            def load_next_x(b):
                sp.wait_ge(mix_done, HC * (b + 1))
                sp.wait_ge(xbeta_ready, b + 1)
                sp.dma_start(x_cur[:, :, :], x_v[:, bass.ds((b + 1) * TB, TB), :]).then_inc(x_loaded, 16)

            def store_block(b, tiles=TB):
                for t in range(tiles):
                    sp.wait_ge(final_done, TB * b + t + 1)
                    sp.dma_start(out_v[:, bass.ds(b * TB + t, 1), :],
                                 out_buf[:, t:t + 1, :]).then_inc(stored[t], 16)

            with sp.Fori(0, NBLK - 1) as b:
                load_next_x(b)
                store_block(b)
            store_block(NBLK - 1, TB - 1)
            for half in (0, 1):
                cols = slice(half * HID // 2, (half + 1) * HID // 2)
                sp.wait_ge(final_done, NT + half)
                sp.dma_start(out_v[:, NT - 1:NT, cols], out_buf[:, TB - 1:TB, cols]).then_inc(stored[TB - 1], 16)
            for t in range(TB - 1):
                sp.wait_ge(stored[t], 16 * NBLK)
            sp.wait_ge(stored[TB - 1], 16 * (NBLK + 1))

        @block.gpsimd
        def _(pool):
            nc.gpsimd.memset(ident[:, :], 0.0).then_inc(zeroed, 1)
            pool.wait_ge(zeroed, 1)
            nc.gpsimd.affine_select(out=ident[:, :], in_=ident[:, :], compare_op=ALU.not_equal, fill=1.0,
                                    base=0, pattern=[[-1, P]], channel_multiplier=1).then_inc(const_ready, 1)
            nc.gpsimd.memset(mix[:, :, :], 0.0).then_inc(const_ready, 1)
            nc.gpsimd.memset(half[:, :], -0.5).then_inc(const_ready, 1)
            pool.wait_ge(fc1_hi_ready, 1)
            nc.gpsimd.tensor_tensor(fc1_lo[:, :, :], fc1_raw, fc1_hi[:, :, :].bitcast(fp32),
                                    ALU.subtract).then_inc(fc1_lo_ready, 1)
            pool.wait_ge(gate_hi_ready, 1)
            nc.gpsimd.tensor_tensor(gate_hl[:, :, NE:2 * NE], gate_raw, gate_hl[:, :, 0:NE].bitcast(fp32),
                                    ALU.subtract).then_inc(gate_lo_ready, 1)
            pool.wait_ge(agg_act, 2 * G)
            pool.wait_ge(agg_dve, 2 * G)

            def next_mix(b):
                pool.wait_ge(mix_done, HC * (b + 1))
                pool.wait_ge(xbeta_ready, b + 1)
                for g in range(G):
                    if g > 0:
                        pool.wait_ge(mix_ready, G * b + g)
                    r = slice(g * C, (g + 1) * C)
                    nc.gpsimd.tensor_copy(mix[r, :, r], agg[r, bass.ds((b + 1) * TB, TB), :]).then_inc(mix_ready, 1)

            def x_plus_beta(b):
                pool.wait_ge(x_loaded, 16 * (b + 1))
                wait_past(pool, final_done, TB * b)
                nc.gpsimd.tensor_tensor(x_beta, x_cur[:, :, :],
                                        beta_b.unsqueeze(1).to_broadcast([P, TB, HID]),
                                        ALU.add).then_inc(xbeta_ready, 1)

            def inverse_deviations(b):
                for t in range(TB):
                    pool.wait_ge(mv_done, 2 * (TB * b + t + 1))
                    nc.gpsimd.tensor_tensor(rstd[:, :], mv[:, 1:2], half[:, :], ALU.pow).then_inc(rstd_done, 1)

            pool.wait_ge(affine_loaded, 16)
            pool.wait_ge(down_hi_ready, 2)
            pool.wait_ge(down_lo_ready, 2)
            def pool_block(b):
                x_plus_beta(b)
                next_mix(b)
                pool.wait_ge(mix_ready, G * (b + 1))
                inverse_deviations(b)

            pool_block(0)
            with pool.Fori(1, NBLK - 1) as b:
                pool_block(b)
            x_plus_beta(NBLK - 1)
            inverse_deviations(NBLK - 1)

        @block.scalar
        def _(act):
            act.wait_ge(dve_const, 1)
            nc.scalar.activation(warm[:, :], warm[:, :], ACT.Gelu).then_inc(warmed, 1)
            act.wait_ge(mlp_loaded, 16)
            act.wait_ge(h1_done, 1)
            nc.scalar.activation(hid1[:, :], H1, ACT.Gelu, bias=b0_sb).then_inc(gelu_done, 1)
            act.wait_ge(h2_done, 1)
            nc.scalar.activation(hid2[:, :], H2, ACT.Gelu, bias=b1_sb).then_inc(gelu_done, 1)
            act.wait_ge(warmed, 1)
            nc.scalar.activation(warm[:, :], warm[:, :], ACT.Exp).then_inc(warmed, 1)
            act.wait_ge(logit_done, 1)
            act.wait_ge(max_done, 1)
            nc.scalar.activation(att_exp[:, :], LOGIT, ACT.Exp, bias=neg_max[:, :],
                                 accum_out=exp_sum[:, :]).then_inc(exp_done, 1)

            def split_up(i):
                cols = slice(i * UPC, (i + 1) * UPC)
                act.wait_ge(up_loaded[i], 16)
                nc.scalar.copy(up_hi[:, :, cols], up_raw[:, :, cols]).then_inc(up_hi_ready, 1)

            def q_high(lc):
                act.wait_ge(q_done, lc + 1)
                nc.scalar.copy(q_hi[:, lc, :], Q[lc]).then_inc(q_hi_ready, 1)

            def mix_high(b, chunks=range(HC)):
                for c in chunks:
                    act.wait_ge(h_ready, HC * b + c + 1)
                    nc.scalar.copy(h_hi[:, c, :], h_full[:, c % 2, :]).then_inc(h_hi_ready, 1)

            act.wait_ge(const_ready, 2)
            act.wait_ge(agg_done, 1)
            for q in (0, 1):
                for g in range(G):
                    nc.scalar.copy(mix_part(g, q), agg_src(q, g, TB)).then_inc(mix0_act, 1)
            split_up(0)
            act.wait_ge(aggb_done, 1)
            nc.scalar.copy(agg_b[:, 0:TOK], AGG_B).then_inc(aggb_copied, 1)
            act.wait_ge(rows_done, 1)
            nc.scalar.copy(aggb_rows[:, :], AGGB_ROWS).then_inc(rows_copied, 1)
            split_up(1)
            mix_high(0, [0])
            mix_high(0, [1, 2, 3])
            split_up(2)
            split_up(3)
            for q in (0, 1):
                for g in range(G):
                    nc.scalar.copy(agg_part(g, q), agg_src(q, g, NT)).then_inc(agg_act, 1)
            act.wait_ge(latents_loaded, 16)
            nc.scalar.copy(fc1_hi[:, :, :], fc1_raw).then_inc(fc1_hi_ready, 1)
            act.wait_ge(dve_const, 2)
            nc.scalar.copy(gate_hl[:, :, 0:NE], gate_raw).then_inc(gate_hi_ready, 1)

            def relu_square(b, m):
                act.wait_ge(up_done, IC * b + m + 1)
                wait_past(act, sq_lo_ready, IC * b + max(m - 1, 0))
                nc.scalar.activation(relu_sq[:, m % 2, :], ps[:, UP_BANK[m], :], ACT.Relu).then_inc(relu_done, 1)
                act.wait_ge(relu_done, IC * b + m + 1)
                nc.scalar.activation(relu_sq[:, m % 2, :], relu_sq[:, m % 2, :], ACT.Square).then_inc(square_done, 1)

            def latent_gate(b):
                for lc in range(LC):
                    act.wait_ge(lat_done, LC * b + lc + 1)
                    nc.scalar.copy(lat_hi[:, lc, :], ps[:, LAT_BANK[lc], :]).then_inc(lat_hi_ready, 1)
                act.wait_ge(gate_done, b + 1)
                nc.scalar.copy(gate_sb, ps[0:2 * NE, GATE_BANK, :]).then_inc(gate_copied, 1)

            def scale_routed(b):
                act.wait_ge(top2_done, b + 1)
                for t in range(TB):
                    act.wait_ge(routed_done, TB * b + t + 1)
                    wait_past(act, final_done, TB * b + max(t - 1, 0))
                    nc.scalar.mul(y_buf[:, t % 2, :], routed(t), top2[:, t:t + 1]).then_inc(scaled_done, 1)

            def down_high(i):
                ks = slice(i * DNC, (i + 1) * DNC)
                act.wait_ge(down_loaded[i], 16)
                nc.scalar.copy(down_hi[:, ks, :], down_raw[:, ks, :]).then_inc(down_hi_ready, 1)

            for m in range(IC):
                relu_square(0, m)
                if m in (0, 1):
                    q_high(m)
                if m in (2, 3, 4, 5):
                    down_high(m - 2)
            latent_gate(0)
            mix_high(1)
            scale_routed(0)
            with act.Fori(1, NBLK - 1) as b:
                for m in range(IC):
                    relu_square(b, m)
                latent_gate(b)
                mix_high(b + 1)
                scale_routed(b)
            for m in range(IC):
                relu_square(NBLK - 1, m)
            latent_gate(NBLK - 1)
            scale_routed(NBLK - 1)

        @block.vector
        def _(dve):
            nc.vector.memset(warm[:, :], 0.0).then_inc(dve_const, 1)
            nc.vector.memset(gate_hl[:, :, :].bitcast(mybir.dt.uint32), 0).then_inc(dve_const, 1)
            nc.vector.memset(ones[:, :].bitcast(mybir.dt.uint32), ONE_BITS).then_inc(dve_const, 1)
            dve.wait_ge(kernels_loaded, 16)
            nc.vector.tensor_copy(weight_parts, weight_raw).then_inc(weight_hi_ready, 1)
            dve.wait_ge(weight_hi_ready, 1)
            nc.vector.tensor_tensor(weight_parts[LAST, :], weight_raw[LAST, :], weight_parts[LAST, :].bitcast(fp32),
                                    ALU.subtract).then_inc(weight_lo_ready, 1)
            dve.wait_ge(logit_done, 1)
            nc.vector.tensor_reduce(neg_max[:, :], LOGIT, AX.X, ALU.max, negate=True).then_inc(max_done, 1)
            dve.wait_ge(exp_done, 1)
            nc.vector.reciprocal(exp_inv[:, :], exp_sum[:, :]).then_inc(inv_done, 1)
            dve.wait_ge(inv_done, 1)
            nc.vector.tensor_scalar(att.rearrange("b (g k) -> b g k", k=K),
                                    att_exp[:, :].unsqueeze(1).to_broadcast([NB, SR // K, K]),
                                    exp_inv[:, :], None, ALU.mult).then_inc(att_done, 1)
            dve.wait_ge(attT_done, 1)
            nc.vector.tensor_copy(att_parts[:, :], ATT_T).then_inc(att_hi_ready, 1)
            dve.wait_ge(att_hi_ready, 1)
            nc.vector.tensor_tensor(att_parts[FIRST, :], ATT_T[FIRST, :], att_parts[FIRST, :].bitcast(fp32),
                                    ALU.subtract).then_inc(att_lo_ready, 1)
            nc.vector.tensor_copy(att_T[:, :], ATT_T[0:2 * K, :]).then_inc(attT_copied, 1)
            dve.wait_ge(attT_copied, 1)
            nc.vector.tensor_tensor(
                att_bias.rearrange("k (b o) -> k b o", o=C),
                att_T[:, 0:TOK // C].unsqueeze(2).to_broadcast([2 * K, TOK // C, C]),
                bias_raw[0:2 * K, :].unsqueeze(1).to_broadcast([2 * K, TOK // C, C]),
                ALU.mult).then_inc(attb_ready, 1)
            dve.wait_ge(attb_ready, 1)
            nc.vector.tensor_copy(bias_parts, att_bias).then_inc(attb_hi_ready, 1)
            dve.wait_ge(attb_hi_ready, 1)
            nc.vector.tensor_tensor(bias_parts[FIRST, :], att_bias[FIRST, :], bias_parts[FIRST, :].bitcast(fp32),
                                    ALU.subtract).then_inc(attb_lo_ready, 1)

            def split_up(m, n=1):
                cols = slice(m * P, (m + n) * P)
                dve.wait_ge(up_hi_ready, (m + n - 1) * P // UPC + 1)
                nc.vector.tensor_tensor(up_lo[:, :, cols], up_raw[:, :, cols],
                                        up_hi[:, :, cols].bitcast(fp32), ALU.subtract).then_inc(up_lo_ready, n)

            def q_low(lc):
                dve.wait_ge(q_hi_ready, lc + 1)
                nc.vector.tensor_tensor(q_lo[:, lc, :], Q[lc], q_hi[:, lc, :].bitcast(fp32),
                                        ALU.subtract).then_inc(q_lo_ready, 1)

            def mix_bias(b, c):
                dve.wait_ge(mix_done, HC * b + c + 1)
                bank = MIX0_BANK[c] if isinstance(b, int) and b == 0 else MIX_BANK[c]
                wait_past(dve, h_hi_ready, HC * b + max(c - 1, 0))
                wait_past(dve, h_lo_ready, HC * b + max(c - 1, 0))
                nc.vector.tensor_tensor(h_full[:, c % 2, :], ps[:, bank, :],
                                        agg_b[:, bass.ds(b * TOK, TOK)], ALU.add).then_inc(h_ready, 1)

            def mix_low(b, c):
                dve.wait_ge(h_hi_ready, HC * b + c + 1)
                nc.vector.tensor_tensor(h_lo[:, c, :], h_full[:, c % 2, :], h_hi[:, c, :].bitcast(fp32),
                                        ALU.subtract).then_inc(h_lo_ready, 1)

            dve.wait_ge(const_ready, 2)
            dve.wait_ge(agg_done, 1)
            for q in (2, 3):
                for g in range(G):
                    nc.vector.tensor_copy(mix_part(g, q), agg_src(q, g, TB)).then_inc(mix0_dve, 1)
            split_up(0, 2)
            dve.wait_ge(aggb_copied, 1)
            mix_bias(0, 0)
            split_up(2)
            mix_low(0, 0)
            mix_bias(0, 1)
            split_up(3)
            mix_low(0, 1)
            mix_bias(0, 2)
            mix_low(0, 2)
            mix_bias(0, 3)
            mix_low(0, 3)
            split_up(4, 2)
            split_up(6, 2)
            for q in (2, 3):
                for g in range(G):
                    nc.vector.tensor_copy(agg_part(g, q), agg_src(q, g, NT)).then_inc(agg_dve, 1)
            def split_square(b, m):
                dve.wait_ge(square_done, IC * b + m + 1)
                nc.vector.tensor_copy(sq_hi[:, m, :], relu_sq[:, m % 2, :]).then_inc(sq_hi_ready, 1)
                dve.wait_ge(sq_hi_ready, IC * b + m + 1)
                nc.vector.tensor_tensor(sq_lo[:, m, :], relu_sq[:, m % 2, :], sq_hi[:, m, :].bitcast(fp32),
                                        ALU.subtract).then_inc(sq_lo_ready, 1)

            def latent_low(b):
                for lc in range(LC):
                    dve.wait_ge(lat_hi_ready, LC * b + lc + 1)
                    nc.vector.tensor_tensor(lat_lo[:, lc, :], ps[:, LAT_BANK[lc], :],
                                            lat_hi[:, lc, :].bitcast(fp32), ALU.subtract).then_inc(lat_lo_ready, 1)

            def top_two(b):
                dve.wait_ge(logits_done, b + 1)
                nc.vector.tensor_reduce(logits[:, :, :], TOP, AX.X, ALU.add).then_inc(logits_summed, 1)
                dve.wait_ge(gate_lo_ready, 1)
                dve.wait_ge(logits_summed, b + 1)
                for t in range(TB):
                    nc.vector.max(out=top8[:, t, :], in_=logits[:, t, :]).then_inc(top8_done, 1)
                dve.wait_ge(top8_done, TB * (b + 1))
                nc.vector.tensor_tensor(top2[:, :], top8[:, :, 0], top8[:, :, 1], ALU.add).then_inc(top2_done, 1)

            def normalise(b, t):
                n = TB * b + t + 1
                y = y_buf[:, t % 2, :]
                dve.wait_ge(scaled_done, n)
                dve.wait_ge(shared_done, n)
                nc.vector.tensor_tensor(y, shared(t), y, ALU.add).then_inc(y_done, 1)
                dve.wait_ge(y_done, n)
                nc.vector.bn_stats(out=stats[:, :], in_=y).then_inc(stats_done, 1)
                dve.wait_ge(affine_loaded, 16)
                dve.wait_ge(stats_done, n)
                nc.vector.bn_aggr(out=mv[:, :], in_=stats[:, :]).then_inc(mv_done, 1)
                dve.wait_ge(mv_done, 2 * n - 1)
                nc.vector.tensor_scalar(mv[:, 1:2], mv[:, 1:2], EPS, None, ALU.add).then_inc(mv_done, 1)
                nc.vector.scalar_tensor_tensor(out=y, in0=y, scalar=mv[:, 0:1], in1=gamma_b,
                                               op0=ALU.subtract, op1=ALU.mult).then_inc(gamma_done, 1)
                dve.wait_ge(gamma_done, n)
                dve.wait_ge(rstd_done, n)
                dve.wait_ge(xbeta_ready, b + 1)
                wait_past(dve, stored[t], 16 * b)
                nc.vector.scalar_tensor_tensor(out=out_buf[:, t, :], in0=y, scalar=rstd[:, :],
                                               in1=x_beta[:, t, :], op0=ALU.mult,
                                               op1=ALU.add).then_inc(final_done, 1)

            def normalise_last():
                b, t = NBLK - 1, TB - 1
                n = NT
                y = y_buf[:, t % 2, :]
                halves = [slice(0, HID // 2), slice(HID // 2, HID)]
                dve.wait_ge(scaled_done, n)
                for i, cols in enumerate(halves):
                    dve.wait_ge(shared_done, n + i)
                    nc.vector.tensor_tensor(y[:, cols], last_shared(i), y[:, cols], ALU.add).then_inc(y_done, 1)
                    dve.wait_ge(y_done, n + i)
                    nc.vector.bn_stats(out=last_stats[:, i, :], in_=y[:, cols]).then_inc(stats_done, 1)
                dve.wait_ge(stats_done, n + 1)
                nc.vector.bn_aggr(out=mv[:, :], in_=last_stats[:, :, :]).then_inc(mv_done, 1)
                dve.wait_ge(mv_done, 2 * n - 1)
                nc.vector.tensor_scalar(mv[:, 1:2], mv[:, 1:2], EPS, None, ALU.add).then_inc(mv_done, 1)
                nc.vector.scalar_tensor_tensor(out=y, in0=y, scalar=mv[:, 0:1], in1=gamma_b,
                                               op0=ALU.subtract, op1=ALU.mult).then_inc(gamma_done, 1)
                dve.wait_ge(gamma_done, n)
                dve.wait_ge(rstd_done, n)
                dve.wait_ge(xbeta_ready, b + 1)
                dve.wait_ge(stored[t], 16 * b)
                for cols in halves:
                    nc.vector.scalar_tensor_tensor(out=out_buf[:, t, cols], in0=y[:, cols], scalar=rstd[:, :],
                                                   in1=x_beta[:, t, cols], op0=ALU.mult,
                                                   op1=ALU.add).then_inc(final_done, 1)

            def down_low(i):
                ks = slice(i * DNC, (i + 1) * DNC)
                dve.wait_ge(down_hi_ready, i + 1)
                nc.vector.tensor_tensor(down_lo[:, ks, :], down_raw[:, ks, :], down_hi[:, ks, :].bitcast(fp32),
                                        ALU.subtract).then_inc(down_lo_ready, 1)

            for m in range(IC):
                split_square(0, m)
                if m in (0, 1):
                    q_low(m)
                if m in (2, 3, 4, 5):
                    down_low(m - 2)
            latent_low(0)
            dve.wait_ge(aggb_loaded, 16)
            mix_bias(1, 0)
            mix_bias(1, 1)
            top_two(0)
            mix_low(1, 0)
            mix_bias(1, 2)
            mix_low(1, 1)
            mix_bias(1, 3)
            mix_low(1, 2)
            mix_low(1, 3)
            for t in range(TB):
                normalise(0, t)
            with dve.Fori(1, NBLK - 1) as b:
                for m in range(IC):
                    split_square(b, m)
                latent_low(b)
                mix_bias(b + 1, 0)
                mix_bias(b + 1, 1)
                top_two(b)
                mix_low(b + 1, 0)
                mix_bias(b + 1, 2)
                mix_low(b + 1, 1)
                mix_bias(b + 1, 3)
                mix_low(b + 1, 2)
                mix_low(b + 1, 3)
                for t in range(TB):
                    normalise(b, t)
            for m in range(IC):
                split_square(NBLK - 1, m)
            latent_low(NBLK - 1)
            top_two(NBLK - 1)
            for t in range(TB - 1):
                normalise(NBLK - 1, t)
            normalise_last()

        @block.tensor
        def _(pe):
            def stay_warm(n):
                for i in range(n):
                    nc.tensor.matmul(IDLE, gate_hl[:, 0, :], gate_hl[:, 1:3, :], start=True, stop=True)

            def fold_expert(lc, half, m):
                cols = slice(half * HID // 2, (half + 1) * HID // 2)
                return nc.tensor.matmul(Q[lc][:, cols], expert_T[:, m, lc * P:(lc + 1) * P],
                                        fc2_raw[:, m, cols], start=(m == 0), stop=(m == LC - 1))

            pe.wait_ge(dve_const, 3)
            stay_warm(11)
            pe.wait_ge(mlp_loaded, 16)
            nc.tensor.matmul(H1, w0_sb, cond_T, start=True, stop=True).then_inc(h1_done, 1)
            stay_warm(5)
            pe.wait_ge(gelu_done, 1)
            nc.tensor.matmul(H2, w1_sb, hid1[:, :], start=True, stop=True).then_inc(h2_done, 1)
            stay_warm(4)
            pe.wait_ge(kernels_loaded, 16)
            pe.wait_ge(gelu_done, 2)
            nc.tensor.matmul(LOGIT, hid2[:, :], w2_sb, start=True, stop=False)
            nc.tensor.matmul(LOGIT, ones[0:1, 0:NB].bitcast(fp32), b2_sb, start=False, stop=True).then_inc(logit_done, 1)
            stay_warm(1)
            pe.wait_ge(experts_loaded, 16)
            fold_expert(0, 0, 0)
            stay_warm(1)
            pe.wait_ge(const_ready, 1)
            pe.wait_ge(att_done, 1)
            nc.tensor.transpose(ATT_T, att[:, :], ident[0:NB, 0:NB]).then_inc(attT_done, 1)
            fold_expert(0, 0, 1)
            pe.wait_ge(weight_lo_ready, 1)
            pe.wait_ge(att_lo_ready, 1)
            for c in range(C // G):
                last = nc.tensor.matmul(AGG[:, c, :], weight_parts[:, c * P:(c + 1) * P], att_parts[:, :],
                                        start=True, stop=True)
            last.then_inc(agg_done, 1)

            pe.wait_ge(attT_copied, 1)
            nc.tensor.matmul(AGGB_ROWS, att_T[0:K, :], bias_raw[0:K, :], start=True, stop=True).then_inc(rows_done, 1)
            stay_warm(1)
            pe.wait_ge(attb_lo_ready, 1)
            nc.tensor.matmul(AGG_B, ones[:, :], bias_parts, start=True, stop=True).then_inc(aggb_done, 1)
            stay_warm(3)

            def mix_chunk(b, c, bank):
                for t in range(TB):
                    last = nc.tensor.matmul(ps[:, bank, t * P:(t + 1) * P],
                                            x_cur[:, t, c * P:(c + 1) * P], mix[:, t, :], start=True, stop=True)
                last.then_inc(mix_done, 1)

            pe.wait_ge(x_loaded, 16)
            pe.wait_ge(mix0_act, 2 * G)
            pe.wait_ge(mix0_dve, 2 * G)
            mix_chunk(0, 0, MIX0_BANK[0])
            mix_chunk(0, 1, MIX0_BANK[1])
            pe.wait_ge(h_ready, 1)
            mix_chunk(0, 2, MIX0_BANK[2])
            fold_expert(0, 1, 0)

            def three_products(dst, a_hi, a_lo, b_hi, b_lo, first, last):
                nc.tensor.matmul(dst, a_hi, b_hi, start=first, stop=False)
                nc.tensor.matmul(dst, a_hi, b_lo, start=False, stop=False)
                return nc.tensor.matmul(dst, a_lo, b_hi, start=False, stop=last)

            def up_chunk(m, c):
                cols = slice(m * P, (m + 1) * P)
                return three_products(ps[:, UP_BANK[m], :], up_hi[:, c, cols], up_lo[:, c, cols],
                                      h_hi[:, c, :], h_lo[:, c, :], c == 0, c == HC - 1)

            def up_first_block():
                for c in range(HC):
                    pe.wait_ge(h_hi_ready, c + 1)
                    pe.wait_ge(h_lo_ready, c + 1)
                    for m in range(WB):
                        if c == 0:
                            pe.wait_ge(up_lo_ready, m + 1)
                        if c == 0 and m == 3:
                            pe.wait_ge(rows_copied, 1)
                        last = up_chunk(m, c)
                        if c == HC - 1:
                            last.then_inc(up_done, 1)
                    if c == 0:
                        pe.wait_ge(h_ready, 2)
                        mix_chunk(0, 3, MIX0_BANK[3])
                fold_expert(0, 1, 1).then_inc(q_done, 1)
                pe.wait_ge(h_ready, 3)
                for half in (0, 1):
                    for m in range(LC):
                        last = fold_expert(1, half, m)
                last.then_inc(q_done, 1)
                for m in range(WB, IC):
                    pe.wait_ge(up_lo_ready, m + 1)
                    pe.wait_ge(relu_done, m - WB + 1)
                    for c in range(HC):
                        last = up_chunk(m, c)
                    last.then_inc(up_done, 1)

            def up_product(b):
                for m in range(IC):
                    if m == 1:
                        pe.wait_ge(top2_done, b)
                    if m >= WB:
                        pe.wait_ge(relu_done, IC * b + m - WB + 1)
                    for c in range(HC):
                        if m == 0:
                            pe.wait_ge(h_hi_ready, HC * b + c + 1)
                            pe.wait_ge(h_lo_ready, HC * b + c + 1)
                        last = up_chunk(m, c)
                    last.then_inc(up_done, 1)

            def latent_product(b):
                for lc in range(LC):
                    cols = slice(lc * P, (lc + 1) * P)
                    pe.wait_ge(relu_done, IC * b + WB + lc + 1)
                    for c in range(HC):
                        last = three_products(ps[:, LAT_BANK[lc], :], fc1_hi[:, c, cols], fc1_lo[:, c, cols],
                                              h_hi[:, c, :], h_lo[:, c, :], c == 0, c == HC - 1)
                    last.then_inc(lat_done, 1)

            def gate_product(b):
                pe.wait_ge(relu_done, IC * b + WB + LC + 1)
                for c in range(HC):
                    nc.tensor.matmul(ps[0:GC, GATE_BANK, :], gate_hl[:, c, :], h_hi[:, c, :],
                                     start=(c == 0), stop=False)
                    last = nc.tensor.matmul(ps[0:GC, GATE_BANK, :], gate_hl[:, c, :], h_lo[:, c, :],
                                            start=False, stop=(c == HC - 1))
                last.then_inc(gate_done, 1)

            def wait_for_logits(b):
                pe.wait_ge(lat_lo_ready, LC * b + 2)
                pe.wait_ge(gate_copied, b + 1)

            def logits_to_rows():
                for t in range(TB):
                    last = nc.tensor.transpose(ps[:, TOP_BANK, t * 2 * NE:(t + 1) * 2 * NE],
                                               gate_sb[:, t * P:(t + 1) * P], ident[0:2 * NE, 0:2 * NE])
                last.then_inc(logits_done, 1)

            def down_product(b, first_block=False, last_block=False):
                for t in range(TB):
                    rows = slice(t * P, (t + 1) * P)
                    wait_past(pe, y_done, TB * b + max(t - 1, 0))
                    for lc in range(LC):
                        if t == 0:
                            pe.wait_ge(lat_hi_ready, LC * b + lc + 1)
                            pe.wait_ge(lat_lo_ready, LC * b + lc + 1)
                        last = three_products(routed(t), lat_hi[:, lc, rows], lat_lo[:, lc, rows],
                                              q_hi[:, lc, :], q_lo[:, lc, :], lc == 0, lc == LC - 1)
                    last.then_inc(routed_done, 1)
                    if last_block and t == 0:
                        wait_for_logits(b)
                        logits_to_rows()
                    if first_block and t == 1:
                        pe.wait_ge(agg_act, 2 * G)
                        pe.wait_ge(agg_dve, 2 * G)
                    if last_block and t == TB - 1:
                        for half in (0, 1):
                            cols = slice(half * HID // 2, (half + 1) * HID // 2)
                            for m in range(IC):
                                last = three_products(last_shared(half), sq_hi[:, m, rows], sq_lo[:, m, rows],
                                                      down_hi[:, m, cols], down_lo[:, m, cols],
                                                      m == 0, m == IC - 1)
                            last.then_inc(shared_done, 1)
                        continue
                    for m in range(IC):
                        if t == 0:
                            if first_block and m % DNC == 0:
                                pe.wait_ge(down_lo_ready, m // DNC + 1)
                            pe.wait_ge(sq_lo_ready, IC * b + m + 1)
                        last = three_products(shared(t), sq_hi[:, m, rows], sq_lo[:, m, rows],
                                              down_hi[:, m, :], down_lo[:, m, :], m == 0, m == IC - 1)
                    last.then_inc(shared_done, 1)

            def block_of(b, first_block=False, last_block=False):
                if first_block:
                    up_first_block()
                    pe.wait_ge(fc1_lo_ready, 1)
                else:
                    up_product(b)
                latent_product(b)
                if first_block:
                    pe.wait_ge(gate_lo_ready, 1)
                gate_product(b)
                if not last_block:
                    pe.wait_ge(x_loaded, 16 * (b + 2))
                    pe.wait_ge(mix_ready, G * (b + 1))
                    pe.wait_ge(relu_done, IC * (b + 1))
                    mix_chunk(b + 1, 0, MIX_BANK[0])
                    pe.wait_ge(lat_lo_ready, LC * b + 1)
                    mix_chunk(b + 1, 1, MIX_BANK[1])
                    wait_for_logits(b)
                    mix_chunk(b + 1, 2, MIX_BANK[2])
                    logits_to_rows()
                    pe.wait_ge(h_ready, HC * (b + 1) + 1)
                    mix_chunk(b + 1, 3, MIX_BANK[3])
                down_product(b, first_block, last_block)

            block_of(0, first_block=True)
            with pe.Fori(1, NBLK - 1) as b:
                block_of(b)
            block_of(NBLK - 1, last_block=True)


_OUTS = [((64, 32, 512), 'float32')]


def kernel(x, cond_128, L0_cond_W0, L0_cond_b0, L0_cond_W1, L0_cond_b1, L0_cond_W2, L0_cond_b2, L0_cond_weight,
           L0_cond_bias_k, L0_ffn_gate_w, L0_ffn_up_w, L0_ffn_down_w, L0_ffn_fc1_w, L0_ffn_fc2_w,
           L0_ffn_expert_w, L0_ffn_ln_gamma, L0_ffn_ln_beta):
    import numpy as _np
    import concourse.bacc as _bacc
    from concourse import mybir as _mybir
    from concourse.bass_utils import run_bass_kernel_spmd as _run

    a = [_np.asarray(v) for v in (cond_128, L0_cond_W0, L0_cond_W1, L0_cond_W2, L0_cond_b0, L0_cond_b1)]
    cond, w0, w1, w2, b0, b1 = a
    weight, bias_k, b2 = (_np.asarray(v) for v in (L0_cond_weight, L0_cond_bias_k, L0_cond_b2))
    nk = bias_k.shape[0]
    b2_rows = _np.zeros((nk, nk), b2.dtype)
    b2_rows[0] = b2
    one = _np.concatenate([weight.reshape(nk, -1), bias_k, b2_rows], axis=1)
    stacked = _np.zeros((32 + nk, one.shape[1]), one.dtype)
    for row in (0, nk, 32):
        stacked[row:row + nk] = one
    ins = {
        "x": x,
        "mlp": _np.concatenate([cond.T, w0, w1, w2, b0[:, None], b1[:, None]], axis=1),
        "kernels": stacked,
        "latents": _np.concatenate([_np.asarray(L0_ffn_fc1_w), _np.asarray(L0_ffn_gate_w)], axis=1),
        "experts": _np.concatenate([_np.asarray(L0_ffn_expert_w).T, _np.asarray(L0_ffn_fc2_w)], axis=1),
        "up_w": L0_ffn_up_w,
        "down_w": L0_ffn_down_w,
        "affine": _np.stack([_np.asarray(L0_ffn_ln_gamma), _np.asarray(L0_ffn_ln_beta)]),
    }
    nc = _bacc.Bacc("TRN2", target_bir_lowering=False, num_devices=1)
    arrays, args = {}, []
    for name, value in ins.items():
        v = _np.ascontiguousarray(value)
        arrays[f"in_{name}_dram"] = v
        args.append(nc.dram_tensor(f"in_{name}_dram", v.shape, _mybir.dt.from_np(v.dtype), kind="ExternalInput").ap())
    for i, (shape, dtype) in enumerate(_OUTS):
        dt = _mybir.dt.from_np(_np.dtype(dtype))
        args.append(nc.dram_tensor(f"out_{i}_dram", shape, dt, kind="ExternalOutput").ap())
    adaln_ffn_kernel(nc, *args)
    r = _run(nc, [arrays], core_ids=[0])
    got = tuple(r.results[0][f"out_{i}_dram"] for i in range(len(_OUTS)))
    return got[0]
```
